# Optimizing a Trainium2 kernel written in Bass

```python
import numpy as np
import jax
import jax.numpy as jnp

def _softmax(x, axis=-1):
    return jax.nn.softmax(x, axis=axis)
def _gelu(x):
    return jax.nn.gelu(x, approximate=True)
def _silu(x):
    return jax.nn.silu(x)
def _sigmoid(x):
    return jax.nn.sigmoid(x)
def _layernorm(x, axis=-1, eps=1e-5):
    m = jnp.mean(x, axis=axis, keepdims=True)
    v = jnp.var(x, axis=axis, keepdims=True)
    return (x - m) / jnp.sqrt(v + eps)
def _scatter_add(tgt, idx, src, axis=0):
    return tgt.at[idx].add(src)
def _segment_sum(src, seg, n):
    return jax.ops.segment_sum(src, seg, n)

kernel_name = 'mk_conv_preact_d1_conv_nchw64_527d7d'

def setup_inputs(seed: int = 0):
    np.random.seed(seed)
    _w = jnp.asarray
    def _rec_inputs():
        import jax
        import jax.numpy as jnp
        _gk = jax.random.key(seed)
        x = -7.109e-05 + 0.9999 * jax.random.normal(jax.random.fold_in(_gk, 1), (16, 64, 256, 256), jnp.float32)
        return x
    x = _rec_inputs()
    def _L0_conv_setup():
        import jax, jax.numpy as jnp
        import numpy as np
        EPS = 1e-12

        def cosine_attention(x):
            B, C, H, W = x.shape
            f = x.reshape(B, C, H * W)
            colsum = f.sum(axis=2)
            score = jnp.einsum('bcn,bc->bn', f, colsum)
            norm = jnp.maximum(jnp.linalg.norm(score, axis=1, keepdims=True), EPS)
            return (score / norm).reshape(B, H, W)
        key = jax.random.key(seed)
        k1, k2, k3 = jax.random.split(key, 3)
        B, C, H, W = (16, 64, 256, 256)
        x = jax.random.normal(k1, (B, C, H, W), dtype=jnp.float32)
        pw_w = jax.random.normal(k2, (C, C), dtype=jnp.float32) * (1.0 / np.sqrt(C))
        pw_b = jax.random.normal(k3, (C,), dtype=jnp.float32) * 0.01
        return {'x': x, 'pw_w': pw_w, 'pw_b': pw_b}
    _L0_conv_all = _L0_conv_setup()
    _L0_conv_in = {k: v for k, v in _L0_conv_all.items() if k in ('pw_w', 'pw_b', )}
    del _L0_conv_all

    return {
        "x": x,
        "L0_conv_pw_w": _L0_conv_in["pw_w"],
        "L0_conv_pw_b": _L0_conv_in["pw_b"],
    }

def reference(x, L0_conv_pw_w, L0_conv_pw_b):
    import jax
    import jax.numpy as jnp
    def _L0_conv_ref(x, pw_w, pw_b):
        import jax, jax.numpy as jnp
        import numpy as np
        EPS = 1e-12

        def cosine_attention(x):
            B, C, H, W = x.shape
            f = x.reshape(B, C, H * W)
            colsum = f.sum(axis=2)
            score = jnp.einsum('bcn,bc->bn', f, colsum)
            norm = jnp.maximum(jnp.linalg.norm(score, axis=1, keepdims=True), EPS)
            return (score / norm).reshape(B, H, W)
        s = cosine_attention(x)
        y = jnp.einsum('bchw,oc->bohw', x, pw_w) + pw_b[None, :, None, None]
        s_ = cosine_attention(y)
        raise_sp = jax.nn.softmax(s_ - s, axis=0)
        att_score = jax.nn.sigmoid(s_ * (1.0 + raise_sp))[:, None, :, :]
        return y * att_score

    def _gn(v, G=32, eps=1e-5):
        B_, C_, H_, W_ = v.shape
        g = v.reshape(B_, G, C_ // G, H_, W_)
        m = jnp.mean(g, axis=(2, 3, 4), keepdims=True)
        s = jnp.var(g, axis=(2, 3, 4), keepdims=True)
        return ((g - m) / jnp.sqrt(s + eps)).reshape(v.shape)

    def _ln_c(v, eps=1e-6):
        m = jnp.mean(v, axis=1, keepdims=True)
        s = jnp.var(v, axis=1, keepdims=True)
        return (v - m) / jnp.sqrt(s + eps)

    def _ln_t(v, eps=1e-5):
        m = jnp.mean(v, axis=-1, keepdims=True)
        s = jnp.var(v, axis=-1, keepdims=True)
        return (v - m) / jnp.sqrt(s + eps)

    def _to_tokens(v):
        B_, C_, H_, W_ = v.shape
        return v.reshape(B_, C_, H_ * W_).transpose(0, 2, 1)
    def _from_tokens(t, like):
        B_, C_, H_, W_ = like.shape
        return t.transpose(0, 2, 1).reshape(B_, C_, H_, W_)

    x = x + _L0_conv_ref(_gn(x), L0_conv_pw_w, L0_conv_pw_b)
    return x


_drawn_inputs = setup_inputs


def setup_inputs(seed=0):
    import zlib

    import numpy as np

    out = dict(_drawn_inputs(seed))
    spreads = {}
    factors = {'L0_conv_pw_b': 8.0}
    for name, (base, spread) in spreads.items():
        noise = np.random.default_rng([zlib.crc32(name.encode()), seed]).standard_normal(out[name].shape)
        drawn = base * np.exp(spread * noise) if base else spread * noise
        out[name] = jnp.asarray(drawn.astype(out[name].dtype))
    for name, factor in factors.items():
        out[name] = (out[name] * factor).astype(out[name].dtype)
    return out
```

```python
from contextlib import ExitStack

import concourse.bass as bass
from concourse import mybir

F32 = mybir.dt.float32
F16 = mybir.dt.float16
ALU = mybir.AluOpType
ACT = mybir.ActivationFunctionType
AX_X = mybir.AxisListType.X

P = 128
GN_EPS = 1e-5
NORM_EPS = 1e-12
ATT_SCALE = 4096.0


def at_least(eng, sem, value):
    if isinstance(value, int) and value <= 0:
        return
    eng.wait_ge(sem, value)


def build_kernel(nc, x, w, w_t, bias, masks, gate_select, out):
    B, C, H, W = x.shape
    N = H * W
    PAIRS = B // 2
    QUAD = 32
    QUADS = P // QUAD
    CH = C // QUAD

    RUN = 1024
    TILE_PX = QUADS * RUN
    IN_SLOTS = 4
    ROUND_PX = IN_SLOTS * TILE_PX
    ROUNDS = N // ROUND_PX
    HALF_ROUNDS = ROUNDS // 2
    BLOCKS = RUN // QUAD
    XT_SLOTS = 2
    XT_ROW = C + 2
    G = C + 1

    PIECE = 1024
    PART = PIECE // QUADS
    PIECES = N // PIECE
    SLOTS = 4
    PB = PART // QUAD
    BANK = 512
    HALVES = PIECE // BANK
    STORE_PAIRS = 2
    STORES = PAIRS // STORE_PAIRS
    DMA = 16

    x_bc = x.rearrange("b (e c) h w -> b c e (h w)", e=CH)
    x_rows = x.rearrange("b c h w -> (b c) (h w)").rearrange("(p r) n -> r p n", r=P)
    out_rows = out.rearrange("b c h w -> (b c) (h w)").rearrange("(p r) n -> r p n", r=P)

    with ExitStack() as ctx:
        def sb(name, shape, dt=F32):
            return ctx.enter_context(nc.sbuf_tensor(name, shape, dt))

        def sem(name):
            return ctx.enter_context(nc.semaphore(name))

        piece_x = sb("piece_x", [P, SLOTS, PAIRS, PIECE])
        tiles_in = piece_x[:, SLOTS - 1, :, :].rearrange("q (s e) n -> q s e n", s=IN_SLOTS)
        x_t = sb("x_t", [P, XT_SLOTS, BLOCKS, XT_ROW])
        gram_kept_sb = sb("gram_kept_sb", [P, B, 2, G])
        gram = sb("gram", [P, PAIRS, G])
        gram_diag = sb("gram_diag", [P, PAIRS, C])
        zeros = sb("zeros", [P, G])

        NM = C + 5 * P + 1
        masks_sb = sb("masks_sb", [P, NM])
        eye = masks_sb[:, 0:C]
        same_channel = masks_sb[:, C:C + P]
        same_group = masks_sb[:, C + P:C + 2 * P]
        same_image = masks_sb[:, C + 2 * P:C + 3 * P]
        row_of_image = [masks_sb[:, C + (3 + h) * P:C + (4 + h) * P] for h in range(2)]
        first_row = masks_sb[:, C + 5 * P:C + 5 * P + 1]
        select = sb("select", [P, QUADS, PAIRS, P], F16)
        w_pair = sb("w_pair", [P, P])
        wt_pair = sb("wt_pair", [P, P])
        b_col = sb("b_col", [P, 1])
        b_times_n = sb("b_times_n", [P, 1])

        sum_sq = sb("sum_sq", [P, 2, PAIRS])
        mean_sq = sb("mean_sq", [P, 2, PAIRS])
        mean = mean_sq[:, 0, :]
        var = sb("var", [P, PAIRS])
        std = sb("std", [P, PAIRS])
        rstd0 = sb("rstd0", [P, PAIRS])
        newton = sb("newton", [P, 2, PAIRS])
        rstd = sb("rstd", [P, PAIRS])
        conv_in = sb("conv_in", [P, 2, PAIRS])
        cy = sb("cy", [P, PAIRS])
        conv_b = sb("conv_b", [P, PAIRS])
        sw = sb("sw", [P, 2, PAIRS])
        parts = sb("parts", [P, 6, PAIRS])
        totals = sb("totals", [P, 6, PAIRS])
        sk = sb("sk", [P, 2, PAIRS])
        sk_sq = sb("sk_sq", [P, 2, PAIRS])
        cross = sb("cross", [P, 2, PAIRS])
        norm2 = sb("norm2", [P, 2, PAIRS])
        norm = sb("norm", [P, 2, PAIRS])
        inv0 = sb("inv0", [P, 2, PAIRS])
        inv = sb("inv", [P, 2, PAIRS])
        swk = sb("swk", [P, 2, 2, PAIRS])
        dwk = sb("dwk", [P, 2, 2, PAIRS])
        k_row = sb("k_row", [P, 2 * B])
        k_rows = sb("k_rows", [P, QUADS, 2 * B])
        score_b = sb("score_b", [P, 1])
        score_w = sb("score_w", [P, PAIRS * 2 * B])
        conv_w = sb("conv_w", [P, PAIRS, P])

        y_sb = sb("y_sb", [P, 2, PIECE])
        score_rows = sb("score_rows", [P, PART])
        scores = sb("scores", [P, PB, 2 * B])
        e_sb = sb("e_sb", [P, PB, B])
        z_sb = sb("z_sb", [P, PB])
        rz_sb = sb("rz_sb", [P, PB])
        p_sb = sb("p_sb", [P, PB, B])
        g_sb = sb("g_sb", [P, PB, B])
        tanh_sb = sb("tanh_sb", [P, PB, B])
        gate4k = sb("gate4k", [P, PB, B])
        gate_parts = sb("gate_parts", [P, PB, 2 * B], F16)
        gate_rows = sb("gate_rows", [P, 2, PB * 2 * B], F16)

        banks = ctx.enter_context(nc.psum_tensor("banks", [P, 8, BANK], F32))
        gram_ps = [banks[:, h, 0:G] for h in range(2)]
        scores_ps = banks[:, 7, 0:PART]
        y_ps = [banks[:, 5 + k, :] for k in range(HALVES)]
        gate_ps = [banks[:, 1 + 2 * g:3 + 2 * g, :].rearrange("q a n -> q (a n)") for g in range(2)]

        masks_loaded = sem("masks_loaded")
        weights_loaded = sem("weights_loaded")
        select_loaded = sem("select_loaded")
        cleared = sem("cleared")
        tile_loaded = [sem(f"tile_loaded{i}") for i in range(IN_SLOTS)]
        tile_turned = sem("tile_turned")
        tile_summed = sem("tile_summed")
        gram_ended = sem("gram_ended")
        gram_kept = sem("gram_kept")
        pe_coef = sem("pe_coef")
        act_coef = sem("act_coef")
        dve_coef = sem("dve_coef")
        piece_loaded = [sem(f"piece_loaded{i}") for i in range(SLOTS)]
        piece_stored = [sem(f"piece_stored{i}") for i in range(SLOTS)]
        scores_summed = sem("scores_summed")
        rows_ready = sem("rows_ready")
        scores_ready = sem("scores_ready")
        exp_ready = sem("exp_ready")
        soft = sem("soft")
        tanh_ready = sem("tanh_ready")
        high_ready = sem("high_ready")
        split = sem("split")
        gate_ready = sem("gate_ready")
        conv_done = sem("conv_done")
        y_ready = sem("y_ready")
        gate_spread = sem("gate_spread")
        gated = sem("gated")
        added = sem("added")

        PE_STEPS = ["gram", "groups", "conv", "back", "forms", "totals", "constants", "score_b"]
        ACT_STEPS = ["std", "conv_w", "norm"]
        pe_at = {name: n + 1 for n, name in enumerate(PE_STEPS)}
        act_at = {name: n + 1 for n, name in enumerate(ACT_STEPS)}
        DVE_STEPS = [
            "b_times_n", "gram_0", "gram_1", "diag", "sums", "squares",
            "mean_sq", "mean2", "var", "var_eps", "rstd0", "r_sq", "r_sq_v", "r_fix", "rstd",
            "rm", "centred", "colsum", "cy", "conv_b", "sw_x", "sw_y",
            "part_0", "part_1", "part_sums", "part_forms_0", "part_forms_1",
            "totals", "sk_x", "sk_y", "sk_sq", "cross", "cross2", "norm2", "norm2_held",
            "inv0", "i_sq", "i_sq_n", "i_fix", "inv", "sw_n", "sk_n", "differences", "kept",
            "score_w_0", "score_w_1", "score_w_2", "score_w_3", "k_row", "k_rows", "score_b",
        ]
        dve_at = {name: n + 1 for n, name in enumerate(DVE_STEPS)}

        block = ctx.enter_context(nc.Block())

        @block.sync
        def _(sp):
            def load_round(image, quarter, rnd):
                for u in range(IN_SLOTS):
                    at_least(sp, tile_turned, IN_SLOTS * (rnd - 1) + u + 1)
                    for j in range(QUADS):
                        first = quarter * ROUND_PX + u * TILE_PX + j * RUN
                        sp.dma_start(
                            tiles_in[j * QUAD:(j + 1) * QUAD, u, :, :],
                            x_bc[image, :, :, first:first + RUN] if isinstance(image, int)
                            else x_bc[bass.ds(image, 1), :, :, first:first + RUN].rearrange("b c e n -> (b c) e n"),
                        ).then_inc(tile_loaded[u], DMA)

            def load_piece(first, slot):
                for g in range(STORES):
                    pairs = slice(g * STORE_PAIRS, (g + 1) * STORE_PAIRS)
                    sp.dma_start(piece_x[:, slot, pairs, :],
                                 x_rows[:, pairs, bass.ds(first, PIECE)]).then_inc(piece_loaded[slot], DMA)

            def pieces(i, last):
                for u in range(SLOTS):
                    for g in range(STORES):
                        at_least(sp, added, i * (SLOTS * PAIRS) + (u * PAIRS + (g + 1) * STORE_PAIRS))
                        pairs = slice(g * STORE_PAIRS, (g + 1) * STORE_PAIRS)
                        sp.dma_start(out_rows[:, pairs, bass.ds(i * (SLOTS * PIECE) + u * PIECE, PIECE)],
                                     piece_x[:, u, pairs, :]).then_inc(piece_stored[u], DMA)
                        if g == 0 and not (last and u > 0):
                            before = (u - 1) % SLOTS
                            at_least(sp, piece_stored[before],
                                     i * (STORES * DMA) + (STORES * DMA if u > 0 else 0))
                            load_piece(i * (SLOTS * PIECE) + (u + SLOTS - 1) * PIECE, before)

            load_round(0, 0, 0)
            sp.dma_start(masks_sb[:, :], masks).then_inc(masks_loaded, DMA)
            sp.wait_ge(cleared, 4)
            for h in range(2):
                half = slice(h * C, (h + 1) * C)
                sp.dma_start(w_pair[half, half], w).then_inc(weights_loaded, DMA)
                sp.dma_start(wt_pair[half, half], w_t).then_inc(weights_loaded, DMA)
                sp.dma_start(b_col[half, :], bias).then_inc(weights_loaded, DMA)
            for quarter in range(1, ROUNDS):
                load_round(0, quarter, quarter)
            with sp.Fori(1, B) as image:
                for quarter in range(ROUNDS):
                    load_round(image, quarter, image * ROUNDS + quarter)
            sp.dma_start(select[:, :, :, :].rearrange("q a b c -> q (a b c)"), gate_select).then_inc(select_loaded, DMA)
            for s in range(SLOTS - 1):
                load_piece(s * PIECE, s)
            sp.wait_ge(tile_turned, B * ROUNDS * IN_SLOTS)
            pieces(0, False)
            with sp.Fori(1, PIECES // SLOTS - 1) as i:
                pieces(i, False)
            pieces(PIECES // SLOTS - 1, True)
            for u in range(SLOTS):
                sp.wait_ge(piece_stored[u], (PIECES // SLOTS) * STORES * DMA)

        @block.gpsimd
        def _(pool):
            nc.gpsimd.memset(zeros[:, :], 0.0).then_inc(cleared, 1)
            nc.gpsimd.memset(x_t[:, :, :, C:XT_ROW], 1.0).then_inc(cleared, 1)
            nc.gpsimd.memset(w_pair[:, :], 0.0).then_inc(cleared, 1)
            nc.gpsimd.memset(wt_pair[:, :], 0.0).then_inc(cleared, 1)
            nc.gpsimd.memset(score_w[:, :], 0.0).then_inc(cleared, 1)

        @block.tensor
        def _(pe):
            def open_or_close(h, opens):
                for half in range(2):
                    rows = slice(half * C, (half + 1) * C)
                    last = nc.tensor.matmul(gram_ps[h][rows, :], zeros[:, 0:C], zeros[:, :],
                                            start=opens, stop=not opens, skip_group_check=True)
                return last

            def gram_tiles(h, first_tile):
                for u in range(IN_SLOTS):
                    at_least(pe, tile_turned, first_tile + u + 1)
                    for j in range(BLOCKS):
                        half = j % 2
                        block_x = x_t[:, u % XT_SLOTS, j, :]
                        last = nc.tensor.matmul(gram_ps[h][half * C:(half + 1) * C, :], block_x[:, 0:C],
                                                block_x[:, 0:G], start=False, stop=False,
                                                skip_group_check=True)
                    last.then_inc(tile_summed, 1)

            pe.wait_ge(cleared, 2)
            def image_gram(image):
                for h in range(2):
                    at_least(pe, gram_kept, image * 2 + h - 1)
                    open_or_close(h, True)
                    with pe.Fori(0, HALF_ROUNDS) as r:
                        gram_tiles(h, image * (ROUNDS * IN_SLOTS) + h * (HALF_ROUNDS * IN_SLOTS) + r * IN_SLOTS)
                    open_or_close(h, False).then_inc(gram_ended, 1)

            image_gram(0)
            with pe.Fori(1, B) as image:
                image_gram(image)

            pe.wait_ge(masks_loaded, DMA)
            pe.wait_ge(weights_loaded, 6 * DMA)
            pe.wait_ge(gram_kept, 2 * B)
            for q in range(B // 4):
                for h in range(2):
                    last = nc.tensor.matmul(banks[:, 2 + q, 0:4 * G], same_channel,
                                            gram_kept_sb[:, 4 * q:4 * q + 4, h, :], start=(h == 0), stop=(h == 1))
            last.then_inc(pe_coef, 1)
            pe.wait_ge(dve_coef, dve_at["squares"])
            nc.tensor.matmul(banks[:, 6, 0:2 * PAIRS], same_group, sum_sq[:, :, :].rearrange("q t p -> q (t p)"),
                             start=True, stop=True).then_inc(pe_coef, 1)
            pe.wait_ge(dve_coef, dve_at["colsum"])
            nc.tensor.matmul(banks[:, 7, 0:2 * PAIRS], wt_pair[:, :], conv_in[:, :, :].rearrange("q t p -> q (t p)"),
                             start=True, stop=True).then_inc(pe_coef, 1)
            pe.wait_ge(dve_coef, dve_at["cy"])
            nc.tensor.matmul(banks[:, 6, 0:PAIRS], w_pair[:, :], cy[:, :], start=True, stop=True).then_inc(pe_coef, 1)
            pe.wait_ge(dve_coef, dve_at["sw_y"])
            for h in range(2):
                rows = slice(h * C, (h + 1) * C)
                for p in range(PAIRS):
                    last = nc.tensor.matmul(banks[rows, 2 + h, 2 * p:2 * p + 2], gram[rows, p, 0:C],
                                            sw[rows, :, p], start=True, stop=True)
            last.then_inc(pe_coef, 1)
            pe.wait_ge(dve_coef, dve_at["part_forms_1"])
            nc.tensor.matmul(banks[:, 4, 0:6 * PAIRS], same_image, parts[:, :, :].rearrange("q t p -> q (t p)"),
                             start=True, stop=True).then_inc(pe_coef, 1)
            pe.wait_ge(dve_coef, dve_at["kept"])
            for h in range(2):
                last = nc.tensor.matmul(banks[:, 5, 2 * PAIRS * h:2 * PAIRS * (h + 1)], row_of_image[h],
                                        dwk[:, 1, :, :].rearrange("q t p -> q (t p)"), start=True, stop=True)
            last.then_inc(pe_coef, 1)
            pe.wait_ge(dve_coef, dve_at["k_rows"])
            nc.tensor.matmul(banks[:, 6, 0:1], k_rows[:, :, :].rearrange("q j r -> q (j r)"), first_row,
                             start=True, stop=True).then_inc(pe_coef, 1)

            def sum_scores(i, u):
                at_least(pe, piece_loaded[u % SLOTS], i * (STORES * DMA) + STORES * DMA * (u // SLOTS + 1))
                at_least(pe, rows_ready, i * SLOTS + u)
                for p in range(PAIRS):
                    for j in range(QUADS):
                        last = nc.tensor.matmul(scores_ps[j * QUAD:(j + 1) * QUAD, :],
                                                score_w[:, p * 2 * B:(p + 1) * 2 * B],
                                                piece_x[:, u % SLOTS, p, j * PART:(j + 1) * PART],
                                                start=(p == 0), stop=(p == PAIRS - 1))
                last.then_inc(scores_summed, 1)

            def pieces(i, last_pieces):
                for u in range(SLOTS):
                    for p in range(PAIRS):
                        n = u * PAIRS + p
                        for k in range(HALVES):
                            at_least(pe, y_ready, i * (SLOTS * PAIRS * HALVES) + (n - 1) * HALVES + k + 1)
                            nc.tensor.matmul(y_ps[k], conv_w[:, p, :], piece_x[:, u, p, k * BANK:(k + 1) * BANK],
                                             start=True, stop=True).then_inc(conv_done, 1)
                        if p == 0:
                            at_least(pe, gate_ready, i * SLOTS + u + 1)
                        at_least(pe, added, i * (SLOTS * PAIRS) + n - 1)
                        for j in range(QUADS):
                            last = nc.tensor.matmul(gate_ps[n % 2][:, j * PART:(j + 1) * PART], select[:, j, p, :],
                                                    gate_rows[:, u % 2, :], start=True, stop=True)
                        last.then_inc(gate_spread, 1)
                        if p == 0 and not (last_pieces and u == SLOTS - 1):
                            sum_scores(i, u + 1)

            pe.wait_ge(dve_coef, dve_at["score_b"])
            pe.wait_ge(act_coef, act_at["norm"])
            sum_scores(0, 0)
            pe.wait_ge(select_loaded, DMA)
            pieces(0, False)
            with pe.Fori(1, PIECES // SLOTS - 1) as i:
                pieces(i, False)
            pieces(PIECES // SLOTS - 1, True)

        @block.scalar
        def _(act):
            with act.Fori(0, B) as image:
                for h in range(2):
                    act.wait_ge(gram_ended, image * 2 + h + 1)
                    nc.scalar.copy(gram_kept_sb[:, bass.ds(image, 1), h, :].rearrange("q b g -> q (b g)"),
                                   gram_ps[h]).then_inc(gram_kept, 1)

            act.wait_ge(dve_coef, dve_at["var_eps"])
            nc.scalar.activation(std[:, :], var[:, :], ACT.Sqrt).then_inc(act_coef, 1)
            act.wait_ge(dve_coef, dve_at["rstd"])
            act.wait_ge(weights_loaded, 6 * DMA)
            for p in range(PAIRS):
                last = nc.scalar.activation(conv_w[:, p, :], wt_pair[:, :], ACT.Copy, scale=rstd[:, p:p + 1])
            last.then_inc(act_coef, 1)
            act.wait_ge(dve_coef, dve_at["norm2_held"])
            nc.scalar.activation(norm[:, :, :], norm2[:, :, :], ACT.Sqrt).then_inc(act_coef, 1)

            def score_rows_out(n):
                at_least(act, scores_summed, n + 1)
                nc.scalar.activation(score_rows[:, :], scores_ps, ACT.Identity, bias=score_b[:, 0:1],
                                     scale=1.0).then_inc(rows_ready, 1)

            def exponentials(n):
                at_least(act, scores_ready, n + 1)
                nc.scalar.activation(e_sb[:, :, :], scores[:, :, 0:B], ACT.Exp).then_inc(exp_ready, 1)

            def gate_out(n):
                at_least(act, soft, n * 4 + 4)
                nc.scalar.activation(tanh_sb[:, :, :], g_sb[:, :, :], ACT.Tanh, scale=0.5).then_inc(tanh_ready, 1)
                at_least(act, tanh_ready, n + 1)
                nc.scalar.activation(gate_parts[:, :, 0:B], tanh_sb[:, :, :], ACT.Copy, bias=ATT_SCALE / 2,
                                     scale=ATT_SCALE / 2).then_inc(high_ready, 1)

            def pieces(i, last_pieces):
                for u in range(SLOTS):
                    following = i * SLOTS + u + 1
                    more = not (last_pieces and u == SLOTS - 1)
                    for p in range(PAIRS):
                        n = u * PAIRS + p
                        at_least(act, gated, i * (SLOTS * PAIRS) + n - 1)
                        for k in range(HALVES):
                            at_least(act, conv_done, i * (SLOTS * PAIRS * HALVES) + n * HALVES + k + 1)
                            nc.scalar.activation(y_sb[:, n % 2, k * BANK:(k + 1) * BANK], y_ps[k], ACT.Identity,
                                                 bias=conv_b[:, p:p + 1], scale=1.0).then_inc(y_ready, 1)
                        if more and p == 0:
                            score_rows_out(following)
                        if more and p == 2:
                            exponentials(following)
                        if more and p == 4:
                            gate_out(following)

            act.wait_ge(dve_coef, dve_at["score_b"])
            score_rows_out(0)
            exponentials(0)
            gate_out(0)
            pieces(0, False)
            with act.Fori(1, PIECES // SLOTS - 1) as i:
                pieces(i, False)
            pieces(PIECES // SLOTS - 1, True)

        @block.vector
        def _(dve):
            def turn_round(rnd):
                for u in range(IN_SLOTS):
                    at_least(dve, tile_loaded[u], rnd * (QUADS * DMA) + QUADS * DMA)
                    at_least(dve, tile_summed, rnd * IN_SLOTS + u + 1 - XT_SLOTS)
                    nc.vector.transpose(
                        x_t[:, u % XT_SLOTS, :, 0:C].rearrange("q j (e c) -> q j e c", e=CH),
                        tiles_in[:, u, :, :].rearrange("q e (j n) -> q j e n", n=QUAD)).then_inc(tile_turned, 1)

            turn_round(0)
            with dve.Fori(1, B * ROUNDS) as rnd:
                turn_round(rnd)

            done = []

            def step(name, instruction):
                done.append(name)
                assert DVE_STEPS[len(done) - 1] == name
                instruction.then_inc(dve_coef, 1)
                dve.wait_ge(dve_coef, len(done))

            tt, ts, stt = nc.vector.tensor_tensor, nc.vector.tensor_scalar, nc.vector.scalar_tensor_tensor
            dve.wait_ge(weights_loaded, 6 * DMA)
            dve.wait_ge(masks_loaded, DMA)
            step("b_times_n", ts(b_times_n[:, :], b_col[:, :], float(N), None, ALU.mult))
            dve.wait_ge(pe_coef, pe_at["gram"])
            for h in range(2):
                rows = slice(h * C, (h + 1) * C)
                src = banks[rows, 2:2 + B // 4, 0:4 * G].rearrange("q a (e h g) -> q a e h g", h=2, g=G)[:, :, :, h, :]
                step(f"gram_{h}", nc.vector.tensor_copy(
                    gram[rows, :, :].rearrange("q (a e) g -> q a e g", e=2), src))
            step("diag", tt(gram_diag[:, :, :], gram[:, :, 0:C], eye.unsqueeze(1).to_broadcast([P, PAIRS, C]), ALU.mult))
            step("sums", nc.vector.tensor_copy(sum_sq[:, 0, :], gram[:, :, C]))
            step("squares", nc.vector.tensor_reduce(sum_sq[:, 1, :], gram_diag[:, :, :], AX_X, ALU.add))
            dve.wait_ge(pe_coef, pe_at["groups"])
            step("mean_sq", ts(mean_sq[:, :, :].rearrange("q t p -> q (t p)"), banks[:, 6, 0:2 * PAIRS],
                               1.0 / (2 * N), None, ALU.mult))
            step("mean2", tt(newton[:, 0, :], mean, mean, ALU.mult))
            step("var", tt(var[:, :], mean_sq[:, 1, :], newton[:, 0, :], ALU.subtract))
            step("var_eps", ts(var[:, :], var[:, :], 0.0, GN_EPS, ALU.max, ALU.add))

            def inverse_root(first, names, root, value, scratch, result):
                step(names[0], nc.vector.reciprocal(first, root))
                step(names[1], tt(scratch, first, first, ALU.mult))
                step(names[2], tt(scratch, scratch, value, ALU.mult))
                step(names[3], ts(scratch, scratch, -0.5, 1.5, ALU.mult, ALU.add))
                step(names[4], tt(result, first, scratch, ALU.mult))

            dve.wait_ge(act_coef, act_at["std"])
            inverse_root(rstd0[:, :], ["rstd0", "r_sq", "r_sq_v", "r_fix", "rstd"], std[:, :], var[:, :],
                         newton[:, 0, :], rstd[:, :])
            step("rm", tt(conv_in[:, 1, :], rstd[:, :], mean, ALU.mult))
            step("centred", stt(out=newton[:, 1, :], in0=mean, scalar=-float(N), in1=sum_sq[:, 0, :],
                                op0=ALU.mult, op1=ALU.add))
            step("colsum", tt(conv_in[:, 0, :], newton[:, 1, :], rstd[:, :], ALU.mult))
            dve.wait_ge(pe_coef, pe_at["conv"])
            step("cy", ts(cy[:, :], banks[:, 7, 0:PAIRS], b_times_n[:, 0:1], None, ALU.add))
            step("conv_b", ts(conv_b[:, :], banks[:, 7, PAIRS:2 * PAIRS], -1.0, b_col[:, 0:1], ALU.mult, ALU.add))
            step("sw_x", tt(sw[:, 0, :], conv_in[:, 0, :], rstd[:, :], ALU.mult))
            dve.wait_ge(pe_coef, pe_at["back"])
            step("sw_y", tt(sw[:, 1, :], banks[:, 6, 0:PAIRS], rstd[:, :], ALU.mult))
            step("part_0", tt(parts[:, 0, :], sw[:, 0, :], mean, ALU.mult))
            step("part_1", tt(parts[:, 1, :], cy[:, :], conv_b[:, :], ALU.mult))
            step("part_sums", tt(parts[:, 2:4, :], sw[:, :, :],
                                 sum_sq[:, 0, :].unsqueeze(1).to_broadcast([P, 2, PAIRS]), ALU.mult))
            dve.wait_ge(pe_coef, pe_at["forms"])
            for h in range(2):
                rows = slice(h * C, (h + 1) * C)
                step(f"part_forms_{h}", tt(parts[rows, 4:6, :], sw[rows, :, :],
                                           banks[rows, 2 + h, 0:2 * PAIRS].rearrange("q (p t) -> q t p", t=2),
                                           ALU.mult))
            dve.wait_ge(pe_coef, pe_at["totals"])
            step("totals", nc.vector.tensor_copy(totals[:, :, :].rearrange("q t p -> q (t p)"),
                                                 banks[:, 4, 0:6 * PAIRS]))
            step("sk_x", ts(sk[:, 0, :], totals[:, 0, :], -1.0, None, ALU.mult))
            step("sk_y", nc.vector.tensor_copy(sk[:, 1, :], totals[:, 1, :]))
            step("sk_sq", tt(sk_sq[:, :, :], sk[:, :, :], sk[:, :, :], ALU.mult))
            step("cross", tt(cross[:, :, :], sk[:, :, :], totals[:, 2:4, :], ALU.mult))
            step("cross2", stt(out=cross[:, :, :], in0=cross[:, :, :], scalar=2.0, in1=totals[:, 4:6, :],
                               op0=ALU.mult, op1=ALU.add))
            step("norm2", stt(out=norm2[:, :, :], in0=sk_sq[:, :, :], scalar=float(N), in1=cross[:, :, :],
                              op0=ALU.mult, op1=ALU.add))
            step("norm2_held", ts(norm2[:, :, :], norm2[:, :, :], NORM_EPS ** 2, None, ALU.max))
            dve.wait_ge(act_coef, act_at["norm"])
            inverse_root(inv0[:, :, :], ["inv0", "i_sq", "i_sq_n", "i_fix", "inv"], norm[:, :, :], norm2[:, :, :],
                         newton[:, :, :], inv[:, :, :])
            step("sw_n", tt(swk[:, 0, :, :], sw[:, :, :], inv[:, :, :], ALU.mult))
            step("sk_n", tt(swk[:, 1, :, :], sk[:, :, :], inv[:, :, :], ALU.mult))
            step("differences", tt(dwk[:, :, 0, :], swk[:, :, 1, :], swk[:, :, 0, :], ALU.subtract))
            step("kept", nc.vector.tensor_copy(dwk[:, :, 1, :], swk[:, :, 1, :]))
            dve.wait_ge(cleared, 5)
            for t in range(2):
                for h in range(2):
                    rows, at = slice(h * C, (h + 1) * C), t * B + h
                    step(f"score_w_{2 * t + h}", nc.vector.tensor_copy(score_w[rows, at:PAIRS * 2 * B:2 * B + 2],
                                                                       dwk[rows, 0, t, :]))
            dve.wait_ge(pe_coef, pe_at["constants"])
            step("k_row", nc.vector.tensor_copy(
                k_row[:, :].rearrange("q (t p h) -> q t p h", t=2, h=2),
                banks[:, 5, 0:2 * B].rearrange("q (h t p) -> q t p h", h=2, t=2)))
            step("k_rows", nc.vector.tensor_copy(k_rows[:, :, :],
                                                 k_row[:, :].unsqueeze(1).to_broadcast([P, QUADS, 2 * B])))
            dve.wait_ge(pe_coef, pe_at["score_b"])
            step("score_b", nc.vector.tensor_copy(score_b[:, :], banks[:, 6, 0:1]))

            def scores_by_pixel(n):
                at_least(dve, rows_ready, n + 1)
                nc.vector.transpose(scores[:, :, :].rearrange("q i r -> q (i r)"),
                                    score_rows[:, :]).then_inc(scores_ready, 1)

            def softmax(n):
                at_least(dve, exp_ready, n + 1)
                nc.vector.tensor_reduce(z_sb[:, :], e_sb[:, :, :], AX_X, ALU.add).then_inc(soft, 1)
                at_least(dve, soft, n * 4 + 1)
                nc.vector.reciprocal(rz_sb[:, :], z_sb[:, :]).then_inc(soft, 1)
                at_least(dve, soft, n * 4 + 2)
                tt(p_sb[:, :, :], e_sb[:, :, :], rz_sb[:, :].unsqueeze(2).to_broadcast([P, PB, B]),
                   ALU.mult).then_inc(soft, 1)
                at_least(dve, soft, n * 4 + 3)
                stt(out=g_sb[:, :, :], in0=p_sb[:, :, :], scalar=1.0, in1=scores[:, :, B:2 * B],
                    op0=ALU.add, op1=ALU.mult).then_inc(soft, 1)

            def whole_gate(n):
                at_least(dve, tanh_ready, n + 1)
                ts(gate4k[:, :, :], tanh_sb[:, :, :], ATT_SCALE / 2, ATT_SCALE / 2,
                   ALU.mult, ALU.add).then_inc(split, 1)

            def gate_by_row(n, parity):
                at_least(dve, split, n * 2 + 1)
                at_least(dve, high_ready, n + 1)
                tt(gate_parts[:, :, B:2 * B], gate4k[:, :, :], gate_parts[:, :, 0:B],
                   ALU.subtract).then_inc(split, 1)
                at_least(dve, split, n * 2 + 2)
                nc.vector.transpose(gate_rows[:, parity, :],
                                    gate_parts[:, :, :].rearrange("q i r -> q (i r)")).then_inc(gate_ready, 1)

            def pieces(i, last_pieces):
                for u in range(SLOTS):
                    following = i * SLOTS + u + 1
                    more = not (last_pieces and u == SLOTS - 1)

                    def gate(p):
                        n = u * PAIRS + p
                        at_least(dve, y_ready, i * (SLOTS * PAIRS * HALVES) + (n + 1) * HALVES)
                        at_least(dve, gate_spread, i * (SLOTS * PAIRS) + n + 1)
                        tt(gate_ps[n % 2], y_sb[:, n % 2, :], gate_ps[n % 2], ALU.mult).then_inc(gated, 1)

                    def add(p):
                        n = u * PAIRS + p
                        at_least(dve, gated, i * (SLOTS * PAIRS) + n + 1)
                        tt(piece_x[:, u, p, :], gate_ps[n % 2], piece_x[:, u, p, :], ALU.add).then_inc(added, 1)

                    for p in range(PAIRS):
                        gate(p)
                        if p > 0:
                            add(p - 1)
                        if more and p == 2:
                            scores_by_pixel(following)
                        if more and p == 4:
                            softmax(following)
                        if more and p == 5:
                            whole_gate(following)
                            gate_by_row(following, (u + 1) % 2)
                    add(PAIRS - 1)

            scores_by_pixel(0)
            softmax(0)
            whole_gate(0)
            gate_by_row(0, 0)
            pieces(0, False)
            with dve.Fori(1, PIECES // SLOTS - 1) as i:
                pieces(i, False)
            pieces(PIECES // SLOTS - 1, True)


def masks_of_shape(np, B, C):
    P, QUAD = 128, 32
    row, col = np.arange(P)[:, None], np.arange(P)[None, :]
    eye = (row % C == np.arange(C)[None, :])
    same_channel = row % C == col % C
    same_group = row // 2 == col // 2
    same_image = row // C == col // C
    rows = [np.broadcast_to(row == h * C, (P, P)) for h in range(2)]
    masks = np.concatenate([eye, same_channel, same_group, same_image, *rows, row == 0], axis=1)
    select = np.zeros((P, P // QUAD, B // 2, P), np.float16)
    for j in range(P // QUAD):
        for p in range(B // 2):
            for h in range(2):
                for part in range(2):
                    select[j * QUAD + part * B + 2 * p + h, j, p, h * C:(h + 1) * C] = 1.0 / 4096.0
    return masks.astype(np.float32), select.reshape(P, -1)


def kernel(**inputs):
    import numpy as _np
    import concourse.bacc as _bacc
    from concourse import mybir as _mybir
    from concourse.bass_utils import run_bass_kernel_spmd as _run

    nc = _bacc.Bacc("TRN2", target_bir_lowering=False, num_devices=1)
    x = _np.ascontiguousarray(inputs["x"])
    w = _np.ascontiguousarray(inputs["L0_conv_pw_w"])
    masks, select = masks_of_shape(_np, x.shape[0], x.shape[1])
    arrays = {
        "in_x": x,
        "in_w": w,
        "in_w_t": _np.ascontiguousarray(w.T),
        "in_b": _np.ascontiguousarray(inputs["L0_conv_pw_b"]).reshape(-1, 1),
        "in_masks": masks,
        "in_select": select,
    }
    args = [nc.dram_tensor(n, a.shape, _mybir.dt.from_np(a.dtype), kind="ExternalInput").ap()
            for n, a in arrays.items()]
    out = nc.dram_tensor("out_0", x.shape, _mybir.dt.from_np(x.dtype), kind="ExternalOutput").ap()
    build_kernel(nc, *args, out)
    r = _run(nc, [arrays], core_ids=[0])
    return r.results[0]["out_0"]
```

```python
from contextlib import ExitStack

import concourse.bass as bass
from concourse import mybir

F32 = mybir.dt.float32
F16 = mybir.dt.float16
ALU = mybir.AluOpType
ACT = mybir.ActivationFunctionType
AX_X = mybir.AxisListType.X

P = 128
GN_EPS = 1e-5
NORM_EPS = 1e-12
ATT_SCALE = 4096.0


def at_least(eng, sem, value):
    if isinstance(value, int) and value <= 0:
        return
    eng.wait_ge(sem, value)


def build_kernel(nc, x, w, w_t, bias, masks, gate_select, out):
    B, C, H, W = x.shape
    N = H * W
    PAIRS = B // 2
    QUAD = 32
    QUADS = P // QUAD
    CH = C // QUAD

    RUN = 1024
    TILE_PX = QUADS * RUN
    IN_SLOTS = 4
    ROUND_PX = IN_SLOTS * TILE_PX
    ROUNDS = N // ROUND_PX
    HALF_ROUNDS = ROUNDS // 2
    BLOCKS = RUN // QUAD
    XT_SLOTS = 2
    XT_ROW = 2 * C + 2
    G = C + 1
    GW = 2 * C + 1

    PIECE = 1024
    PART = PIECE // QUADS
    PIECES = N // PIECE
    SLOTS = 4
    PB = PART // QUAD
    BANK = 512
    HALVES = PIECE // BANK
    Y_SLOTS = 4
    STORE_PAIRS = 2
    STORES = PAIRS // STORE_PAIRS
    SCORES_AFTER = {0: range(0, 4), 1: range(4, 8)}
    ROWS_AFTER, EXP_AFTER, TANH_AFTER = 1, 4, 6
    TURN_AFTER, SOFTMAX_AFTER, GATE_AFTER = 1, 3, 5
    DMA = 16

    x_bc = x.rearrange("b (e c) h w -> b c e (h w)", e=CH)
    x_rows = x.rearrange("b c h w -> (b c) (h w)").rearrange("(p r) n -> r p n", r=P)
    out_rows = out.rearrange("b c h w -> (b c) (h w)").rearrange("(p r) n -> r p n", r=P)

    with ExitStack() as ctx:
        def sb(name, shape, dt=F32):
            return ctx.enter_context(nc.sbuf_tensor(name, shape, dt))

        def sem(name):
            return ctx.enter_context(nc.semaphore(name))

        piece_x = sb("piece_x", [P, SLOTS, PAIRS, PIECE])
        tiles_in = sb("tiles_in", [P, IN_SLOTS, CH, RUN])
        turned_or_y = sb("turned_or_y", [P, max(XT_SLOTS * (BLOCKS // 2) * XT_ROW, Y_SLOTS * PIECE)])
        x_t = turned_or_y[:, 0:XT_SLOTS * (BLOCKS // 2) * XT_ROW].rearrange(
            "q (s j c) -> q s j c", s=XT_SLOTS, c=XT_ROW)
        y_sb = turned_or_y[:, 0:Y_SLOTS * PIECE].rearrange("q (s n) -> q s n", s=Y_SLOTS)
        grams_or_select = sb("grams_or_select", [P, max(B * 2 * G, QUADS * PAIRS * P // 2)])
        gram_kept_sb = grams_or_select[:, 0:B * 2 * G].rearrange("q (b h g) -> q b h g", b=B, h=2)
        select = grams_or_select[:, 0:QUADS * PAIRS * P // 2].bitcast(F16).rearrange(
            "q (j p m) -> q j p m", j=QUADS, p=PAIRS)
        gram = sb("gram", [P, PAIRS, G])
        gram_diag = sb("gram_diag", [P, PAIRS, C])
        zeros = sb("zeros", [P, GW])

        NM = C + 5 * P + 1
        masks_sb = sb("masks_sb", [P, NM])
        eye = masks_sb[:, 0:C]
        same_channel = masks_sb[:, C:C + P]
        same_group = masks_sb[:, C + P:C + 2 * P]
        same_image = masks_sb[:, C + 2 * P:C + 3 * P]
        row_of_image = [masks_sb[:, C + (3 + h) * P:C + (4 + h) * P] for h in range(2)]
        first_row = masks_sb[:, C + 5 * P:C + 5 * P + 1]
        w_pair = sb("w_pair", [P, P])
        wt_pair = sb("wt_pair", [P, P])
        b_col = sb("b_col", [P, 1])
        b_times_n = sb("b_times_n", [P, 1])

        sum_sq = sb("sum_sq", [P, 2, PAIRS])
        mean_sq = sb("mean_sq", [P, 2, PAIRS])
        mean = mean_sq[:, 0, :]
        var = sb("var", [P, PAIRS])
        std = sb("std", [P, PAIRS])
        rstd0 = sb("rstd0", [P, PAIRS])
        newton = sb("newton", [P, 2, PAIRS])
        rstd = sb("rstd", [P, PAIRS])
        conv_in = sb("conv_in", [P, 2, PAIRS])
        cy = sb("cy", [P, PAIRS])
        conv_b = sb("conv_b", [P, PAIRS])
        sw = sb("sw", [P, 2, PAIRS])
        parts = sb("parts", [P, 6, PAIRS])
        totals = sb("totals", [P, 6, PAIRS])
        sk = sb("sk", [P, 2, PAIRS])
        sk_sq = sb("sk_sq", [P, 2, PAIRS])
        cross = sb("cross", [P, 2, PAIRS])
        norm2 = sb("norm2", [P, 2, PAIRS])
        norm = sb("norm", [P, 2, PAIRS])
        inv0 = sb("inv0", [P, 2, PAIRS])
        inv = sb("inv", [P, 2, PAIRS])
        swk = sb("swk", [P, 2, 2, PAIRS])
        dwk = sb("dwk", [P, 2, 2, PAIRS])
        k_row = sb("k_row", [P, 2 * B])
        k_rows = sb("k_rows", [P, QUADS, 2 * B])
        score_b = sb("score_b", [P, 1])
        score_w = sb("score_w", [P, PAIRS * 2 * B])
        conv_w = sb("conv_w", [P, PAIRS, P])

        score_rows = sb("score_rows", [P, PART])
        scores = sb("scores", [P, PB, 2 * B])
        e_sb = sb("e_sb", [P, PB, B])
        z_sb = sb("z_sb", [P, PB])
        rz_sb = sb("rz_sb", [P, PB])
        p_sb = sb("p_sb", [P, PB, B])
        g_sb = sb("g_sb", [P, PB, B])
        tanh_sb = sb("tanh_sb", [P, PB, B])
        gate4k = sb("gate4k", [P, PB, B])
        gate_parts = sb("gate_parts", [P, PB, 2 * B], F16)
        gate_rows = sb("gate_rows", [P, 2, PB * 2 * B], F16)

        banks = ctx.enter_context(nc.psum_tensor("banks", [P, 8, BANK], F32))
        gram_ps = [banks[:, h, 0:GW] for h in range(2)]
        scores_ps = banks[:, 7, 0:PART]
        y_ps = [banks[:, 5 + k, :] for k in range(HALVES)]
        gate_ps = [banks[:, 1 + 2 * g:3 + 2 * g, :].rearrange("q a n -> q (a n)") for g in range(2)]

        masks_loaded = sem("masks_loaded")
        weights_loaded = sem("weights_loaded")
        select_loaded = sem("select_loaded")
        cleared = sem("cleared")
        tile_loaded = [sem(f"tile_loaded{i}") for i in range(IN_SLOTS)]
        tile_turned = sem("tile_turned")
        tile_summed = sem("tile_summed")
        gram_ended = sem("gram_ended")
        gram_kept = sem("gram_kept")
        pe_coef = sem("pe_coef")
        act_coef = sem("act_coef")
        dve_coef = sem("dve_coef")
        piece_loaded = [sem(f"piece_loaded{i}") for i in range(SLOTS)]
        group_stored = [[sem(f"group_stored{i}_{g}") for g in range(STORES)] for i in range(SLOTS)]
        scores_summed = sem("scores_summed")
        rows_ready = sem("rows_ready")
        scores_ready = sem("scores_ready")
        exp_ready = sem("exp_ready")
        soft = sem("soft")
        tanh_ready = sem("tanh_ready")
        high_ready = sem("high_ready")
        split = sem("split")
        gate_ready = sem("gate_ready")
        conv_done = sem("conv_done")
        y_ready = sem("y_ready")
        gate_spread = sem("gate_spread")
        gated = sem("gated")
        added = sem("added")

        PE_STEPS = ["gram_early", "gram_late", "groups", "conv", "back", "forms", "totals", "constants", "score_b"]
        ACT_STEPS = ["std", "conv_w", "norm"]
        pe_at = {name: n + 1 for n, name in enumerate(PE_STEPS)}
        act_at = {name: n + 1 for n, name in enumerate(ACT_STEPS)}
        DVE_STEPS = [
            "b_times_n", "gram_0_early", "gram_1_early", "diag_early", "sums_early", "squares_early",
            "gram_0_late", "gram_1_late", "diag_late", "sums_late", "squares_late",
            "mean_sq", "mean2", "var", "var_eps", "rstd0", "r_sq", "r_sq_v", "r_fix", "rstd",
            "rm", "centred", "colsum", "cy", "conv_b", "sw_x", "sw_y",
            "part_0", "part_1", "part_sums", "part_forms_0", "part_forms_1",
            "totals", "sk_x", "sk_y", "sk_sq", "cross", "cross2", "norm2", "norm2_held",
            "inv0", "i_sq", "i_sq_n", "i_fix", "inv", "sw_n", "sk_n", "differences", "kept",
            "score_w_0", "score_w_1", "score_w_2", "score_w_3", "k_row", "k_rows", "score_b",
        ]
        dve_at = {name: n + 1 for n, name in enumerate(DVE_STEPS)}

        block = ctx.enter_context(nc.Block())

        @block.sync
        def _(sp):
            def load_round(image, quarter, rnd):
                for u in range(IN_SLOTS):
                    at_least(sp, tile_turned, IN_SLOTS * (rnd - 1) + u + 1)
                    for j in range(QUADS):
                        first = quarter * ROUND_PX + u * TILE_PX + j * RUN
                        sp.dma_start(
                            tiles_in[j * QUAD:(j + 1) * QUAD, u, :, :],
                            x_bc[image, :, :, first:first + RUN] if isinstance(image, int)
                            else x_bc[bass.ds(image, 1), :, :, first:first + RUN].rearrange("b c e n -> (b c) e n"),
                        ).then_inc(tile_loaded[u], DMA)

            def load_group(first, slot, g):
                pairs = slice(g * STORE_PAIRS, (g + 1) * STORE_PAIRS)
                sp.dma_start(piece_x[:, slot, pairs, :],
                             x_rows[:, pairs, bass.ds(first, PIECE)]).then_inc(piece_loaded[slot], DMA)

            def pieces(i, last):
                for u in range(SLOTS):
                    for g in range(STORES):
                        at_least(sp, added, i * (SLOTS * PAIRS) + (u * PAIRS + (g + 1) * STORE_PAIRS))
                        pairs = slice(g * STORE_PAIRS, (g + 1) * STORE_PAIRS)
                        sp.dma_start(out_rows[:, pairs, bass.ds(i * (SLOTS * PIECE) + u * PIECE, PIECE)],
                                     piece_x[:, u, pairs, :]).then_inc(group_stored[u][g], DMA)
                        slot, group = (u, g - 1) if g > 0 else ((u - 1) % SLOTS, STORES - 1)
                        of_before = g == 0 and u == 0
                        first = (isinstance(i, int) and i == 0)
                        if (first and of_before) or (last and not of_before):
                            continue
                        sp.wait_ge(group_stored[slot][group], i * DMA + (0 if of_before else DMA))
                        load_group(i * (SLOTS * PIECE) + (slot + (0 if of_before else SLOTS)) * PIECE, slot, group)

            load_round(0, 0, 0)
            sp.dma_start(masks_sb[:, :], masks).then_inc(masks_loaded, DMA)
            sp.wait_ge(cleared, 4)
            for h in range(2):
                half = slice(h * C, (h + 1) * C)
                sp.dma_start(w_pair[half, half], w).then_inc(weights_loaded, DMA)
                sp.dma_start(wt_pair[half, half], w_t).then_inc(weights_loaded, DMA)
                sp.dma_start(b_col[half, :], bias).then_inc(weights_loaded, DMA)
            for quarter in range(1, ROUNDS):
                load_round(0, quarter, quarter)
            with sp.Fori(1, B) as image:
                for quarter in range(ROUNDS):
                    load_round(image, quarter, image * ROUNDS + quarter)
            for s in range(SLOTS):
                if s == 1:
                    sp.wait_ge(pe_coef, pe_at["gram_late"])
                    sp.dma_start(select.rearrange("q j p m -> q (j p m)"), gate_select).then_inc(select_loaded, DMA)
                for g in range(STORES):
                    load_group(s * PIECE, s, g)
            pieces(0, False)
            with sp.Fori(1, PIECES // SLOTS - 1) as i:
                pieces(i, False)
            pieces(PIECES // SLOTS - 1, True)
            for u in range(SLOTS):
                for g in range(STORES):
                    sp.wait_ge(group_stored[u][g], (PIECES // SLOTS) * DMA)

        @block.gpsimd
        def _(pool):
            nc.gpsimd.memset(zeros[:, :], 0.0).then_inc(cleared, 1)
            nc.gpsimd.memset(x_t[:, :, :, P:XT_ROW], 1.0).then_inc(cleared, 1)
            nc.gpsimd.memset(w_pair[:, :], 0.0).then_inc(cleared, 1)
            nc.gpsimd.memset(wt_pair[:, :], 0.0).then_inc(cleared, 1)
            nc.gpsimd.memset(score_w[:, :], 0.0).then_inc(cleared, 1)

        @block.tensor
        def _(pe):
            def open_or_close(h, opens):
                return nc.tensor.matmul(gram_ps[h], zeros[:, 0:P], zeros[:, :],
                                        start=opens, stop=not opens, skip_group_check=True)

            def gram_tiles(h, first_tile):
                for u in range(IN_SLOTS):
                    at_least(pe, tile_turned, first_tile + u + 1)
                    for j in range(BLOCKS // 2):
                        two_blocks = x_t[:, u % XT_SLOTS, j, :]
                        last = nc.tensor.matmul(gram_ps[h], two_blocks[:, 0:P], two_blocks[:, 0:GW],
                                                start=False, stop=False, skip_group_check=True)
                    last.then_inc(tile_summed, 1)

            pe.wait_ge(cleared, 2)
            def image_gram(image):
                for h in range(2):
                    at_least(pe, gram_kept, image * 2 + h - 1)
                    open_or_close(h, True)
                    with pe.Fori(0, HALF_ROUNDS) as r:
                        gram_tiles(h, image * (ROUNDS * IN_SLOTS) + h * (HALF_ROUNDS * IN_SLOTS) + r * IN_SLOTS)
                    open_or_close(h, False).then_inc(gram_ended, 1)

            image_gram(0)
            with pe.Fori(1, B - 1) as image:
                image_gram(image)

            def add_parts(fours):
                pe.wait_ge(gram_kept, 2 * 4 * fours[-1] + 8)
                for q in fours:
                    for h in range(2):
                        last = nc.tensor.matmul(banks[:, 2 + q, 0:4 * G], same_channel,
                                                gram_kept_sb[:, 4 * q:4 * q + 4, h, :],
                                                start=(h == 0), stop=(h == 1))
                last.then_inc(pe_coef, 1)

            pe.wait_ge(masks_loaded, DMA)
            pe.wait_ge(weights_loaded, 6 * DMA)
            add_parts(range(B // 4 - 1))
            image_gram(B - 1)
            add_parts([B // 4 - 1])
            pe.wait_ge(dve_coef, dve_at["squares_late"])
            nc.tensor.matmul(banks[:, 6, 0:2 * PAIRS], same_group, sum_sq[:, :, :].rearrange("q t p -> q (t p)"),
                             start=True, stop=True).then_inc(pe_coef, 1)
            pe.wait_ge(dve_coef, dve_at["colsum"])
            nc.tensor.matmul(banks[:, 7, 0:2 * PAIRS], wt_pair[:, :], conv_in[:, :, :].rearrange("q t p -> q (t p)"),
                             start=True, stop=True).then_inc(pe_coef, 1)
            pe.wait_ge(dve_coef, dve_at["cy"])
            nc.tensor.matmul(banks[:, 6, 0:PAIRS], w_pair[:, :], cy[:, :], start=True, stop=True).then_inc(pe_coef, 1)
            pe.wait_ge(dve_coef, dve_at["sw_y"])
            for h in range(2):
                rows = slice(h * C, (h + 1) * C)
                for p in range(PAIRS):
                    last = nc.tensor.matmul(banks[rows, 2 + h, 2 * p:2 * p + 2], gram[rows, p, 0:C],
                                            sw[rows, :, p], start=True, stop=True)
            last.then_inc(pe_coef, 1)
            pe.wait_ge(dve_coef, dve_at["part_forms_1"])
            nc.tensor.matmul(banks[:, 4, 0:6 * PAIRS], same_image, parts[:, :, :].rearrange("q t p -> q (t p)"),
                             start=True, stop=True).then_inc(pe_coef, 1)
            pe.wait_ge(dve_coef, dve_at["kept"])
            for h in range(2):
                last = nc.tensor.matmul(banks[:, 5, 2 * PAIRS * h:2 * PAIRS * (h + 1)], row_of_image[h],
                                        dwk[:, 1, :, :].rearrange("q t p -> q (t p)"), start=True, stop=True)
            last.then_inc(pe_coef, 1)
            pe.wait_ge(dve_coef, dve_at["k_rows"])
            nc.tensor.matmul(banks[:, 6, 0:1], k_rows[:, :, :].rearrange("q j r -> q (j r)"), first_row,
                             start=True, stop=True).then_inc(pe_coef, 1)

            def sum_scores(i, u, pairs):
                if pairs[0] == 0:
                    at_least(pe, piece_loaded[u % SLOTS], i * (STORES * DMA) + STORES * DMA * (u // SLOTS + 1))
                    at_least(pe, rows_ready, i * SLOTS + u)
                for p in pairs:
                    for j in range(QUADS):
                        last = nc.tensor.matmul(scores_ps[j * QUAD:(j + 1) * QUAD, :],
                                                score_w[:, p * 2 * B:(p + 1) * 2 * B],
                                                piece_x[:, u % SLOTS, p, j * PART:(j + 1) * PART],
                                                start=(p == 0), stop=(p == PAIRS - 1))
                if pairs[-1] == PAIRS - 1:
                    last.then_inc(scores_summed, 1)

            def pieces(i, last_pieces):
                for u in range(SLOTS):
                    for p in range(PAIRS):
                        n = u * PAIRS + p
                        for k in range(HALVES):
                            at_least(pe, y_ready, i * (SLOTS * PAIRS * HALVES) + (n - 1) * HALVES + k + 1)
                            nc.tensor.matmul(y_ps[k], conv_w[:, p, :], piece_x[:, u, p, k * BANK:(k + 1) * BANK],
                                             start=True, stop=True).then_inc(conv_done, 1)
                        if p == 0:
                            at_least(pe, gate_ready, i * SLOTS + u + 1)
                        at_least(pe, gated, i * (SLOTS * PAIRS) + n - 1)
                        for j in range(QUADS):
                            last = nc.tensor.matmul(gate_ps[n % 2][:, j * PART:(j + 1) * PART], select[:, j, p, :],
                                                    gate_rows[:, u % 2, :], start=True, stop=True)
                        last.then_inc(gate_spread, 1)
                        if p in SCORES_AFTER and not (last_pieces and u == SLOTS - 1):
                            sum_scores(i, u + 1, SCORES_AFTER[p])

            pe.wait_ge(dve_coef, dve_at["score_b"])
            pe.wait_ge(act_coef, act_at["norm"])
            sum_scores(0, 0, range(PAIRS))
            pe.wait_ge(select_loaded, DMA)
            pieces(0, False)
            with pe.Fori(1, PIECES // SLOTS - 1) as i:
                pieces(i, False)
            pieces(PIECES // SLOTS - 1, True)

        @block.scalar
        def _(act):
            with act.Fori(0, B) as image:
                for h in range(2):
                    act.wait_ge(gram_ended, image * 2 + h + 1)
                    kept = gram_kept_sb[:, bass.ds(image, 1), h, :].rearrange("q b g -> q (b g)")
                    nc.scalar.copy(kept[0:C, 0:C], gram_ps[h][0:C, 0:C])
                    nc.scalar.copy(kept[0:C, C:G], gram_ps[h][0:C, 2 * C:GW])
                    nc.scalar.copy(kept[C:P, :], gram_ps[h][C:P, C:GW]).then_inc(gram_kept, 1)

            act.wait_ge(dve_coef, dve_at["var_eps"])
            nc.scalar.activation(std[:, :], var[:, :], ACT.Sqrt).then_inc(act_coef, 1)
            act.wait_ge(dve_coef, dve_at["rstd"])
            act.wait_ge(weights_loaded, 6 * DMA)
            for p in range(PAIRS):
                last = nc.scalar.activation(conv_w[:, p, :], wt_pair[:, :], ACT.Copy, scale=rstd[:, p:p + 1])
            last.then_inc(act_coef, 1)
            act.wait_ge(dve_coef, dve_at["norm2_held"])
            nc.scalar.activation(norm[:, :, :], norm2[:, :, :], ACT.Sqrt).then_inc(act_coef, 1)

            def score_rows_out(n):
                at_least(act, scores_summed, n + 1)
                nc.scalar.activation(score_rows[:, :], scores_ps, ACT.Identity, bias=score_b[:, 0:1],
                                     scale=1.0).then_inc(rows_ready, 1)

            def exponentials(n):
                at_least(act, scores_ready, n + 1)
                nc.scalar.activation(e_sb[:, :, :], scores[:, :, 0:B], ACT.Exp).then_inc(exp_ready, 1)

            def gate_out(n):
                at_least(act, soft, n * 4 + 4)
                nc.scalar.activation(tanh_sb[:, :, :], g_sb[:, :, :], ACT.Tanh, scale=0.5).then_inc(tanh_ready, 1)
                at_least(act, tanh_ready, n + 1)
                nc.scalar.activation(gate_parts[:, :, 0:B], tanh_sb[:, :, :], ACT.Copy, bias=ATT_SCALE / 2,
                                     scale=ATT_SCALE / 2).then_inc(high_ready, 1)

            def pieces(i, last_pieces):
                for u in range(SLOTS):
                    following = i * SLOTS + u + 1
                    more = not (last_pieces and u == SLOTS - 1)
                    for p in range(PAIRS):
                        n = u * PAIRS + p
                        at_least(act, added, i * (SLOTS * PAIRS) + n + 1 - Y_SLOTS)
                        for k in range(HALVES):
                            at_least(act, conv_done, i * (SLOTS * PAIRS * HALVES) + n * HALVES + k + 1)
                            nc.scalar.activation(y_sb[:, n % Y_SLOTS, k * BANK:(k + 1) * BANK], y_ps[k], ACT.Identity,
                                                 bias=conv_b[:, p:p + 1], scale=1.0).then_inc(y_ready, 1)
                        if more and p == ROWS_AFTER:
                            score_rows_out(following)
                        if more and p == EXP_AFTER:
                            exponentials(following)
                        if more and p == TANH_AFTER:
                            gate_out(following)

            act.wait_ge(dve_coef, dve_at["score_b"])
            score_rows_out(0)
            exponentials(0)
            gate_out(0)
            pieces(0, False)
            with act.Fori(1, PIECES // SLOTS - 1) as i:
                pieces(i, False)
            pieces(PIECES // SLOTS - 1, True)

        @block.vector
        def _(dve):
            def turn_round(rnd):
                for u in range(IN_SLOTS):
                    at_least(dve, tile_loaded[u], rnd * (QUADS * DMA) + QUADS * DMA)
                    at_least(dve, tile_summed, rnd * IN_SLOTS + u + 1 - XT_SLOTS)
                    nc.vector.transpose(
                        x_t[:, u % XT_SLOTS, :, 0:P].rearrange("q j (d e c) -> q j d e c", d=2, e=CH),
                        tiles_in[:, u, :, :].rearrange("q e (j d n) -> q j d e n", d=2, n=QUAD)).then_inc(tile_turned, 1)

            done = []

            def step(name, instruction):
                done.append(name)
                assert DVE_STEPS[len(done) - 1] == name
                instruction.then_inc(dve_coef, 1)
                dve.wait_ge(dve_coef, len(done))

            tt, ts, stt = nc.vector.tensor_tensor, nc.vector.tensor_scalar, nc.vector.scalar_tensor_tensor

            def take_grams(when, first, end):
                dve.wait_ge(pe_coef, pe_at["gram_" + when])
                pairs = slice(2 * first, 2 * end)
                for h in range(2):
                    rows = slice(h * C, (h + 1) * C)
                    src = banks[rows, 2 + first:2 + end, 0:4 * G].rearrange("q a (e h g) -> q a e h g", h=2, g=G)
                    step(f"gram_{h}_{when}", nc.vector.tensor_copy(
                        gram[rows, pairs, :].rearrange("q (a e) g -> q a e g", e=2), src[:, :, :, h, :]))
                step("diag_" + when, tt(gram_diag[:, pairs, :], gram[:, pairs, 0:C],
                                        eye.unsqueeze(1).to_broadcast([P, 2 * (end - first), C]), ALU.mult))
                step("sums_" + when, nc.vector.tensor_copy(sum_sq[:, 0, pairs], gram[:, pairs, C]))
                step("squares_" + when, nc.vector.tensor_reduce(sum_sq[:, 1, pairs], gram_diag[:, pairs, :],
                                                                AX_X, ALU.add))

            turn_round(0)
            with dve.Fori(1, (B - 1) * ROUNDS) as rnd:
                turn_round(rnd)
            turn_round((B - 1) * ROUNDS)
            dve.wait_ge(weights_loaded, 6 * DMA)
            dve.wait_ge(masks_loaded, DMA)
            step("b_times_n", ts(b_times_n[:, :], b_col[:, :], float(N), None, ALU.mult))
            take_grams("early", 0, B // 4 - 1)
            with dve.Fori((B - 1) * ROUNDS + 1, B * ROUNDS) as rnd:
                turn_round(rnd)
            take_grams("late", B // 4 - 1, B // 4)
            dve.wait_ge(pe_coef, pe_at["groups"])
            step("mean_sq", ts(mean_sq[:, :, :].rearrange("q t p -> q (t p)"), banks[:, 6, 0:2 * PAIRS],
                               1.0 / (2 * N), None, ALU.mult))
            step("mean2", tt(newton[:, 0, :], mean, mean, ALU.mult))
            step("var", tt(var[:, :], mean_sq[:, 1, :], newton[:, 0, :], ALU.subtract))
            step("var_eps", ts(var[:, :], var[:, :], 0.0, GN_EPS, ALU.max, ALU.add))

            def inverse_root(first, names, root, value, scratch, result):
                step(names[0], nc.vector.reciprocal(first, root))
                step(names[1], tt(scratch, first, first, ALU.mult))
                step(names[2], tt(scratch, scratch, value, ALU.mult))
                step(names[3], ts(scratch, scratch, -0.5, 1.5, ALU.mult, ALU.add))
                step(names[4], tt(result, first, scratch, ALU.mult))

            dve.wait_ge(act_coef, act_at["std"])
            inverse_root(rstd0[:, :], ["rstd0", "r_sq", "r_sq_v", "r_fix", "rstd"], std[:, :], var[:, :],
                         newton[:, 0, :], rstd[:, :])
            step("rm", tt(conv_in[:, 1, :], rstd[:, :], mean, ALU.mult))
            step("centred", stt(out=newton[:, 1, :], in0=mean, scalar=-float(N), in1=sum_sq[:, 0, :],
                                op0=ALU.mult, op1=ALU.add))
            step("colsum", tt(conv_in[:, 0, :], newton[:, 1, :], rstd[:, :], ALU.mult))
            dve.wait_ge(pe_coef, pe_at["conv"])
            step("cy", ts(cy[:, :], banks[:, 7, 0:PAIRS], b_times_n[:, 0:1], None, ALU.add))
            step("conv_b", ts(conv_b[:, :], banks[:, 7, PAIRS:2 * PAIRS], -1.0, b_col[:, 0:1], ALU.mult, ALU.add))
            step("sw_x", tt(sw[:, 0, :], conv_in[:, 0, :], rstd[:, :], ALU.mult))
            dve.wait_ge(pe_coef, pe_at["back"])
            step("sw_y", tt(sw[:, 1, :], banks[:, 6, 0:PAIRS], rstd[:, :], ALU.mult))
            step("part_0", tt(parts[:, 0, :], sw[:, 0, :], mean, ALU.mult))
            step("part_1", tt(parts[:, 1, :], cy[:, :], conv_b[:, :], ALU.mult))
            step("part_sums", tt(parts[:, 2:4, :], sw[:, :, :],
                                 sum_sq[:, 0, :].unsqueeze(1).to_broadcast([P, 2, PAIRS]), ALU.mult))
            dve.wait_ge(pe_coef, pe_at["forms"])
            for h in range(2):
                rows = slice(h * C, (h + 1) * C)
                step(f"part_forms_{h}", tt(parts[rows, 4:6, :], sw[rows, :, :],
                                           banks[rows, 2 + h, 0:2 * PAIRS].rearrange("q (p t) -> q t p", t=2),
                                           ALU.mult))
            dve.wait_ge(pe_coef, pe_at["totals"])
            step("totals", nc.vector.tensor_copy(totals[:, :, :].rearrange("q t p -> q (t p)"),
                                                 banks[:, 4, 0:6 * PAIRS]))
            step("sk_x", ts(sk[:, 0, :], totals[:, 0, :], -1.0, None, ALU.mult))
            step("sk_y", nc.vector.tensor_copy(sk[:, 1, :], totals[:, 1, :]))
            step("sk_sq", tt(sk_sq[:, :, :], sk[:, :, :], sk[:, :, :], ALU.mult))
            step("cross", tt(cross[:, :, :], sk[:, :, :], totals[:, 2:4, :], ALU.mult))
            step("cross2", stt(out=cross[:, :, :], in0=cross[:, :, :], scalar=2.0, in1=totals[:, 4:6, :],
                               op0=ALU.mult, op1=ALU.add))
            step("norm2", stt(out=norm2[:, :, :], in0=sk_sq[:, :, :], scalar=float(N), in1=cross[:, :, :],
                              op0=ALU.mult, op1=ALU.add))
            step("norm2_held", ts(norm2[:, :, :], norm2[:, :, :], NORM_EPS ** 2, None, ALU.max))
            dve.wait_ge(act_coef, act_at["norm"])
            inverse_root(inv0[:, :, :], ["inv0", "i_sq", "i_sq_n", "i_fix", "inv"], norm[:, :, :], norm2[:, :, :],
                         newton[:, :, :], inv[:, :, :])
            step("sw_n", tt(swk[:, 0, :, :], sw[:, :, :], inv[:, :, :], ALU.mult))
            step("sk_n", tt(swk[:, 1, :, :], sk[:, :, :], inv[:, :, :], ALU.mult))
            step("differences", tt(dwk[:, :, 0, :], swk[:, :, 1, :], swk[:, :, 0, :], ALU.subtract))
            step("kept", nc.vector.tensor_copy(dwk[:, :, 1, :], swk[:, :, 1, :]))
            dve.wait_ge(cleared, 5)
            for t in range(2):
                for h in range(2):
                    rows, at = slice(h * C, (h + 1) * C), t * B + h
                    step(f"score_w_{2 * t + h}", nc.vector.tensor_copy(score_w[rows, at:PAIRS * 2 * B:2 * B + 2],
                                                                       dwk[rows, 0, t, :]))
            dve.wait_ge(pe_coef, pe_at["constants"])
            step("k_row", nc.vector.tensor_copy(
                k_row[:, :].rearrange("q (t p h) -> q t p h", t=2, h=2),
                banks[:, 5, 0:2 * B].rearrange("q (h t p) -> q t p h", h=2, t=2)))
            step("k_rows", nc.vector.tensor_copy(k_rows[:, :, :],
                                                 k_row[:, :].unsqueeze(1).to_broadcast([P, QUADS, 2 * B])))
            dve.wait_ge(pe_coef, pe_at["score_b"])
            step("score_b", nc.vector.tensor_copy(score_b[:, :], banks[:, 6, 0:1]))

            def scores_by_pixel(n):
                at_least(dve, rows_ready, n + 1)
                nc.vector.transpose(scores[:, :, :].rearrange("q i r -> q (i r)"),
                                    score_rows[:, :]).then_inc(scores_ready, 1)

            def softmax(n):
                at_least(dve, exp_ready, n + 1)
                nc.vector.tensor_reduce(z_sb[:, :], e_sb[:, :, :], AX_X, ALU.add).then_inc(soft, 1)
                at_least(dve, soft, n * 4 + 1)
                nc.vector.reciprocal(rz_sb[:, :], z_sb[:, :]).then_inc(soft, 1)
                at_least(dve, soft, n * 4 + 2)
                tt(p_sb[:, :, :], e_sb[:, :, :], rz_sb[:, :].unsqueeze(2).to_broadcast([P, PB, B]),
                   ALU.mult).then_inc(soft, 1)
                at_least(dve, soft, n * 4 + 3)
                stt(out=g_sb[:, :, :], in0=p_sb[:, :, :], scalar=1.0, in1=scores[:, :, B:2 * B],
                    op0=ALU.add, op1=ALU.mult).then_inc(soft, 1)

            def whole_gate(n):
                at_least(dve, tanh_ready, n + 1)
                ts(gate4k[:, :, :], tanh_sb[:, :, :], ATT_SCALE / 2, ATT_SCALE / 2,
                   ALU.mult, ALU.add).then_inc(split, 1)

            def gate_by_row(n, parity):
                at_least(dve, split, n * 2 + 1)
                at_least(dve, high_ready, n + 1)
                tt(gate_parts[:, :, B:2 * B], gate4k[:, :, :], gate_parts[:, :, 0:B],
                   ALU.subtract).then_inc(split, 1)
                at_least(dve, split, n * 2 + 2)
                nc.vector.transpose(gate_rows[:, parity, :],
                                    gate_parts[:, :, :].rearrange("q i r -> q (i r)")).then_inc(gate_ready, 1)

            def pieces(i, last_pieces):
                for u in range(SLOTS):
                    following = i * SLOTS + u + 1
                    more = not (last_pieces and u == SLOTS - 1)

                    def gate(p):
                        n = u * PAIRS + p
                        at_least(dve, y_ready, i * (SLOTS * PAIRS * HALVES) + (n + 1) * HALVES)
                        at_least(dve, gate_spread, i * (SLOTS * PAIRS) + n + 1)
                        tt(y_sb[:, n % Y_SLOTS, :], y_sb[:, n % Y_SLOTS, :], gate_ps[n % 2], ALU.mult).then_inc(gated, 1)

                    def add(p):
                        n = u * PAIRS + p
                        at_least(dve, gated, i * (SLOTS * PAIRS) + n + 1)
                        tt(piece_x[:, u, p, :], y_sb[:, n % Y_SLOTS, :], piece_x[:, u, p, :], ALU.add).then_inc(added, 1)

                    for p in range(PAIRS):
                        gate(p)
                        if p > 0:
                            add(p - 1)
                        if more and p == TURN_AFTER:
                            scores_by_pixel(following)
                        if more and p == SOFTMAX_AFTER:
                            softmax(following)
                        if more and p == GATE_AFTER:
                            whole_gate(following)
                            gate_by_row(following, (u + 1) % 2)
                    add(PAIRS - 1)

            scores_by_pixel(0)
            softmax(0)
            whole_gate(0)
            gate_by_row(0, 0)
            pieces(0, False)
            with dve.Fori(1, PIECES // SLOTS - 1) as i:
                pieces(i, False)
            pieces(PIECES // SLOTS - 1, True)


def masks_of_shape(np, B, C):
    P, QUAD = 128, 32
    row, col = np.arange(P)[:, None], np.arange(P)[None, :]
    eye = (row % C == np.arange(C)[None, :])
    same_channel = row % C == col % C
    same_group = row // 2 == col // 2
    same_image = row // C == col // C
    rows = [np.broadcast_to(row == h * C, (P, P)) for h in range(2)]
    masks = np.concatenate([eye, same_channel, same_group, same_image, *rows, row == 0], axis=1)
    select = np.zeros((P, P // QUAD, B // 2, P), np.float16)
    for j in range(P // QUAD):
        for p in range(B // 2):
            for h in range(2):
                for part in range(2):
                    select[j * QUAD + part * B + 2 * p + h, j, p, h * C:(h + 1) * C] = 1.0 / 4096.0
    return masks.astype(np.float32), select.reshape(P, -1)


def kernel(**inputs):
    import numpy as _np
    import concourse.bacc as _bacc
    from concourse import mybir as _mybir
    from concourse.bass_utils import run_bass_kernel_spmd as _run

    nc = _bacc.Bacc("TRN2", target_bir_lowering=False, num_devices=1)
    x = _np.ascontiguousarray(inputs["x"])
    w = _np.ascontiguousarray(inputs["L0_conv_pw_w"])
    masks, select = masks_of_shape(_np, x.shape[0], x.shape[1])
    arrays = {
        "in_x": x,
        "in_w": w,
        "in_w_t": _np.ascontiguousarray(w.T),
        "in_b": _np.ascontiguousarray(inputs["L0_conv_pw_b"]).reshape(-1, 1),
        "in_masks": masks,
        "in_select": select,
    }
    args = [nc.dram_tensor(n, a.shape, _mybir.dt.from_np(a.dtype), kind="ExternalInput").ap()
            for n, a in arrays.items()]
    out = nc.dram_tensor("out_0", x.shape, _mybir.dt.from_np(x.dtype), kind="ExternalOutput").ap()
    build_kernel(nc, *args, out)
    r = _run(nc, [arrays], core_ids=[0])
    return r.results[0]["out_0"]
```

```python
from contextlib import ExitStack

import concourse.bass as bass
from concourse import mybir

F32 = mybir.dt.float32
F16 = mybir.dt.float16
ALU = mybir.AluOpType
ACT = mybir.ActivationFunctionType
AX_X = mybir.AxisListType.X

P = 128
GN_EPS = 1e-5
NORM_EPS = 1e-12
ATT_SCALE = 4096.0


def at_least(eng, sem, value):
    if isinstance(value, int) and value <= 0:
        return
    eng.wait_ge(sem, value)


def build_kernel(nc, x, w, w_t, bias, masks, gate_select, out):
    B, C, H, W = x.shape
    N = H * W
    PAIRS = B // 2
    QUAD = 32
    QUADS = P // QUAD
    CH = C // QUAD

    RUN = 1024
    TILE_PX = QUADS * RUN
    IN_SLOTS = 3
    ROUND_PX = IN_SLOTS * TILE_PX
    BLOCKS = RUN // QUAD
    XT_SLOTS = IN_SLOTS
    XT_ROW = 2 * C + 2
    G = C + 1
    GW = 2 * C + 1

    PIECE = 1024
    PART = PIECE // QUADS
    PIECES = N // PIECE
    SLOTS = 4
    RESIDENT = SLOTS * PIECE
    GRAM_PX = N - RESIDENT
    ROUNDS = GRAM_PX // ROUND_PX
    HALVES_ROUNDS = [(ROUNDS + 1) // 2, ROUNDS // 2]
    assert ROUNDS * ROUND_PX == GRAM_PX
    PB = PART // QUAD
    BANK = 512
    HALVES = PIECE // BANK
    Y_SLOTS = 4
    STORE_PAIRS = 2
    STORES = PAIRS // STORE_PAIRS
    EXTRA_PAIRS = IN_SLOTS * CH * RUN // PIECE
    EXTRA_GROUPS = EXTRA_PAIRS // STORE_PAIRS
    assert EXTRA_GROUPS * STORE_PAIRS == EXTRA_PAIRS < PAIRS
    SCORES_AFTER = {0: range(0, 4), 1: range(4, 8)}
    ROWS_AFTER, EXP_AFTER, TANH_AFTER = 1, 4, 6
    TURN_AFTER, SOFTMAX_AFTER, GATE_AFTER = 1, 3, 5
    PAIRS_OF = {"early": (0, PAIRS - 2), "late": (PAIRS - 2, PAIRS)}
    EARLY_Y = 2
    DMA = 16

    x_bc = x.rearrange("b (e c) h w -> b c e (h w)", e=CH)
    x_cn = x.rearrange("b c h w -> b c (h w)")
    x_rows = x.rearrange("b c h w -> (b c) (h w)").rearrange("(p r) n -> r p n", r=P)
    out_rows = out.rearrange("b c h w -> (b c) (h w)").rearrange("(p r) n -> r p n", r=P)

    with ExitStack() as ctx:
        def sb(name, shape, dt=F32):
            return ctx.enter_context(nc.sbuf_tensor(name, shape, dt))

        def sem(name):
            return ctx.enter_context(nc.semaphore(name))

        piece_x = sb("piece_x", [P, SLOTS, PAIRS, PIECE])
        tiles_in = sb("tiles_in", [P, IN_SLOTS, CH, RUN])
        turned_or_y = sb("turned_or_y", [P, max(XT_SLOTS * (BLOCKS // 2) * XT_ROW, Y_SLOTS * PIECE)])
        x_t = turned_or_y[:, 0:XT_SLOTS * (BLOCKS // 2) * XT_ROW].rearrange(
            "q (s j c) -> q s j c", s=XT_SLOTS, c=XT_ROW)
        y_sb = turned_or_y[:, 0:Y_SLOTS * PIECE].rearrange("q (s n) -> q s n", s=Y_SLOTS)
        behind_y = [Y_SLOTS * PIECE]

        def gate_sb(shape):
            first = behind_y[0]
            size = 1
            for extent in shape:
                size *= extent
            behind_y[0] += size
            assert behind_y[0] <= XT_SLOTS * (BLOCKS // 2) * XT_ROW
            flat = turned_or_y[:, first:first + size]
            if len(shape) == 1:
                return flat
            return flat.rearrange("q (i r) -> q i r", i=shape[0])

        grams_or_select = sb("grams_or_select", [P, max(B * 2 * G, QUADS * PAIRS * P // 2)])
        gram_kept_sb = grams_or_select[:, 0:B * 2 * G].rearrange("q (b h g) -> q b h g", b=B, h=2)
        select = grams_or_select[:, 0:QUADS * PAIRS * P // 2].bitcast(F16).rearrange(
            "q (j p m) -> q j p m", j=QUADS, p=PAIRS)
        gram = sb("gram", [P, PAIRS, G])
        gram_diag = sb("gram_diag", [P, PAIRS, C])
        zeros = sb("zeros", [P, GW])

        NM = C + 6 * P + 1
        masks_sb = sb("masks_sb", [P, NM])
        eye = masks_sb[:, 0:C]
        same_channel = masks_sb[:, C:C + P]
        same_group = masks_sb[:, C + P:C + 2 * P]
        same_image = masks_sb[:, C + 2 * P:C + 3 * P]
        row_of_image = [masks_sb[:, C + (3 + h) * P:C + (4 + h) * P] for h in range(2)]
        same_score = masks_sb[:, C + 5 * P:C + 6 * P]
        first_row = masks_sb[:, C + 6 * P:C + 6 * P + 1]
        w_pair = sb("w_pair", [P, P])
        wt_pair = sb("wt_pair", [P, P])
        b_col = sb("b_col", [P, 1])
        b_times_n = sb("b_times_n", [P, 1])

        sum_sq = sb("sum_sq", [P, 2, PAIRS])
        mean_sq = sb("mean_sq", [P, 2, PAIRS])
        mean = mean_sq[:, 0, :]
        var = sb("var", [P, PAIRS])
        std = sb("std", [P, PAIRS])
        rstd0 = sb("rstd0", [P, PAIRS])
        newton = sb("newton", [P, 2, PAIRS])
        rstd = sb("rstd", [P, PAIRS])
        conv_in = sb("conv_in", [P, 2, PAIRS])
        cy = sb("cy", [P, PAIRS])
        conv_b = sb("conv_b", [P, PAIRS])
        sw = sb("sw", [P, 2, PAIRS])
        parts = sb("parts", [P, 6, PAIRS])
        totals = sb("totals", [P, 6, PAIRS])
        to_rows = sb("to_rows", [P, 2, 2, PAIRS])
        norm2, sk = to_rows[:, 0, :, :], to_rows[:, 1, :, :]
        sk_sq = sb("sk_sq", [P, 2, PAIRS])
        cross = sb("cross", [P, 2, PAIRS])
        one_row = sb("one_row", [P, 2, 2 * B])
        all_rows = sb("all_rows", [P, 2, QUADS, 2 * B])
        row_k = sb("row_k", [P, 1])
        row_resident = sb("row_resident", [P, 1])
        row_norm2 = sb("row_norm2", [P, 1])
        row_norm = sb("row_norm", [P, 1])
        row_inv0 = sb("row_inv0", [P, 1])
        row_fix = sb("row_fix", [P, 1])
        row_inv = sb("row_inv", [P, 1])
        row_b = sb("row_b", [P, 1])
        score_w = sb("score_w", [P, PAIRS * 2 * B])
        conv_w = sb("conv_w", [P, PAIRS, P])

        resident_stats = sb("resident_stats", [P, 2, PAIRS, SLOTS])
        resident_sum_sq = sb("resident_sum_sq", [P, 2, PAIRS])
        resident_rows = sb("resident_rows", [P, SLOTS, PART])
        resident_norm = sb("resident_norm", [P, SLOTS])
        unused_col = sb("unused_col", [P, 1])
        diff_sb = gate_sb([PB, B])
        score_rows = gate_sb([PART])
        scores = gate_sb([PB, 2 * B])
        e_sb = gate_sb([PB, B])
        z_sb = gate_sb([PB])
        rz_sb = gate_sb([PB])
        p_sb = gate_sb([PB, B])
        g_sb = gate_sb([PB, B])
        tanh_sb = gate_sb([PB, B])
        gate4k = gate_sb([PB, B])
        gate_parts = gate_sb([PB, B]).rearrange("q i r -> q (i r)").bitcast(F16).rearrange(
            "q (i r) -> q i r", i=PB)
        gate_rows = gate_sb([2, PB * B]).rearrange("q k r -> q (k r)").bitcast(F16).rearrange(
            "q (k r) -> q k r", k=2)

        extra_x = tiles_in[:, :, :, :].rearrange("q u e n -> q (u e) n")

        def x_slot(i, u, p):
            if p >= EXTRA_PAIRS or (isinstance(i, int) and i * SLOTS + u < SLOTS):
                return u % SLOTS
            if isinstance(i, int) and i * SLOTS + u == SLOTS:
                return None
            return (u - 1) % SLOTS

        def x_of(i, u, pairs):
            slot = x_slot(i, u, pairs if isinstance(pairs, int) else pairs.start)
            return extra_x[:, pairs, :] if slot is None else piece_x[:, slot, pairs, :]

        banks = ctx.enter_context(nc.psum_tensor("banks", [P, 8, BANK], F32))
        gram_ps = [banks[:, h, 0:GW] for h in range(2)]
        scores_ps = banks[:, 7, 0:PART]
        resident_banks = [banks[:, b, :] for b in (2, 3)]
        resident_ps = [banks[:, 2 + r // 2, r % 2 * PART:(r % 2 + 1) * PART] for r in range(SLOTS)]
        unused_ps = banks[:, 6:8, :].rearrange("q a n -> q (a n)")
        unused_rows_ps = banks[:, 1, 0:PART]
        y_ps = [banks[:, 5 + k, :] for k in range(HALVES)]
        gate_ps = [banks[:, 1 + 2 * g:3 + 2 * g, :].rearrange("q a n -> q (a n)") for g in range(2)]

        masks_loaded = sem("masks_loaded")
        weights_loaded = sem("weights_loaded")
        select_loaded = sem("select_loaded")
        cleared = sem("cleared")
        tile_loaded = [sem(f"tile_loaded{i}") for i in range(IN_SLOTS)]
        tile_turned = sem("tile_turned")
        tile_summed = sem("tile_summed")
        gram_ended = sem("gram_ended")
        gram_kept = sem("gram_kept")
        pe_coef = sem("pe_coef")
        act_coef = sem("act_coef")
        dve_coef = sem("dve_coef")
        piece_loaded = [sem(f"piece_loaded{i}") for i in range(SLOTS)]
        group_stored = [[sem(f"group_stored{i}_{g}") for g in range(STORES)] for i in range(SLOTS)]
        resident_loaded = [sem(f"resident_loaded{h}") for h in range(2)]
        resident_summed = sem("resident_summed")
        resident_out = sem("resident_out")
        resident_squared = sem("resident_squared")
        scores_turned = sem("scores_turned")
        scores_summed = sem("scores_summed")
        rows_ready = sem("rows_ready")
        scores_ready = sem("scores_ready")
        exp_ready = sem("exp_ready")
        soft = sem("soft")
        tanh_ready = sem("tanh_ready")
        high_ready = sem("high_ready")
        split = sem("split")
        gate_ready = sem("gate_ready")
        conv_done = sem("conv_done")
        y_ready = sem("y_ready")
        gate_spread = sem("gate_spread")
        gated = sem("gated")
        added = sem("added")

        PE_STEPS = ["gram_early", "groups_early", "conv_early", "back_early",
                    "gram_late", "groups_late", "conv_late", "back_late", "forms", "totals", "one_row", "rows",
                    "resident"]
        ACT_STEPS = ["std_early", "conv_w_early", "std_late", "conv_w_late", "row_norm"]
        pe_at = {name: n + 1 for n, name in enumerate(PE_STEPS)}
        act_at = {name: n + 1 for n, name in enumerate(ACT_STEPS)}
        weights_steps = [
            "gram_0", "gram_1", "diag", "sums", "squares", "resident_sum_sq", "all_sum_sq",
            "mean_sq", "mean2", "var", "var_eps", "rstd0", "r_sq", "r_sq_v", "r_fix", "rstd",
            "rm", "centred", "colsum", "cy", "conv_b", "sw_x", "sw_y",
            "score_w_0", "score_w_1", "score_w_2", "score_w_3"]
        DVE_STEPS = ["b_times_n"] + [f"{name}_{when}" for when in ("early", "late") for name in weights_steps] + [
            "part_0", "part_1", "part_sums", "part_forms_0", "part_forms_1",
            "totals", "sk_x", "sk_y", "sk_sq", "cross", "cross2", "norm2",
            "one_row_0", "one_row_1", "all_rows", "row_k", "row_resident", "row_norm2", "row_held",
            "inv0", "i_sq", "i_sq_n", "i_fix", "row_inv", "row_b",
        ]
        dve_at = {name: n + 1 for n, name in enumerate(DVE_STEPS)}

        block = ctx.enter_context(nc.Block())

        @block.sync
        def _(sp):
            def load_round(image, quarter, rnd):
                for u in range(IN_SLOTS):
                    at_least(sp, tile_turned, IN_SLOTS * (rnd - 1) + u + 1)
                    for j in range(QUADS):
                        first = RESIDENT + quarter * ROUND_PX + u * TILE_PX + j * RUN
                        sp.dma_start(
                            tiles_in[j * QUAD:(j + 1) * QUAD, u, :, :],
                            x_bc[image, :, :, first:first + RUN] if isinstance(image, int)
                            else x_bc[bass.ds(image, 1), :, :, first:first + RUN].rearrange("b c e n -> (b c) e n"),
                        ).then_inc(tile_loaded[u], DMA)

            def load_resident(pair):
                for h in range(2):
                    at_least(sp, resident_loaded[h], pair * DMA)
                    sp.dma_start(
                        piece_x[h * C:(h + 1) * C, :, bass.ds(pair, 1), :].rearrange("c s p n -> c (s p) n"),
                        x_cn[bass.ds(pair * 2 + h, 1), :, 0:RESIDENT].rearrange("b c (s n) -> (b c) s n", n=PIECE),
                    ).then_inc(resident_loaded[h], DMA)

            def load_group(i, u, g):
                pairs = slice(g * STORE_PAIRS, (g + 1) * STORE_PAIRS)
                first = i * (SLOTS * PIECE) + u * PIECE
                sp.dma_start(x_of(i, u, pairs),
                             x_rows[:, pairs, bass.ds(first, PIECE)]).then_inc(piece_loaded[u % SLOTS], DMA)

            def pieces(i, last):
                for u in range(SLOTS):
                    for g in range(STORES):
                        at_least(sp, added, i * (SLOTS * PAIRS) + (u * PAIRS + (g + 1) * STORE_PAIRS))
                        pairs = slice(g * STORE_PAIRS, (g + 1) * STORE_PAIRS)
                        sp.dma_start(out_rows[:, pairs, bass.ds(i * (SLOTS * PIECE) + u * PIECE, PIECE)],
                                     x_of(i, u, pairs)).then_inc(group_stored[u][g], DMA)
                        stored_u, group = (u, g - 1) if g > 0 else ((u - 1) % SLOTS, STORES - 1)
                        of_before = g == 0 and u == 0
                        first = isinstance(i, int) and i == 0
                        if (first and of_before) or (last and not of_before):
                            continue
                        following = SLOTS
                        if group < EXTRA_GROUPS:
                            if x_slot(i, stored_u, group * STORE_PAIRS) is None:
                                continue
                            if first:
                                following = SLOTS + 1
                        sp.wait_ge(group_stored[stored_u][group], i * DMA + (0 if of_before else DMA))
                        if first and stored_u + following == 2 * SLOTS and group == 0:
                            sp.wait_ge(piece_loaded[0], STORES * DMA)
                        load_group(i, stored_u - (SLOTS if of_before else 0) + following, group)

            load_round(0, 0, 0)
            sp.dma_start(masks_sb[:, :], masks).then_inc(masks_loaded, DMA)
            sp.wait_ge(cleared, 4)
            for h in range(2):
                half = slice(h * C, (h + 1) * C)
                sp.dma_start(w_pair[half, half], w).then_inc(weights_loaded, DMA)
                sp.dma_start(wt_pair[half, half], w_t).then_inc(weights_loaded, DMA)
                sp.dma_start(b_col[half, :], bias).then_inc(weights_loaded, DMA)
            load_resident(0)
            for quarter in range(1, ROUNDS):
                load_round(0, quarter, quarter)
            for quarter in range(ROUNDS):
                load_round(1, quarter, ROUNDS + quarter)
            with sp.Fori(1, PAIRS) as pair:
                load_resident(pair)
                for h in range(2):
                    for quarter in range(ROUNDS):
                        load_round(pair * 2 + h, quarter, pair * (2 * ROUNDS) + h * ROUNDS + quarter)
            sp.wait_ge(tile_turned, B * ROUNDS * IN_SLOTS)
            for g in range(EXTRA_GROUPS):
                load_group(1, 0, g)
            sp.wait_ge(pe_coef, pe_at["gram_late"])
            sp.dma_start(select.rearrange("q j p m -> q (j p m)"), gate_select).then_inc(select_loaded, DMA)
            pieces(0, False)
            pieces(1, False)
            with sp.Fori(2, PIECES // SLOTS - 1) as i:
                pieces(i, False)
            pieces(PIECES // SLOTS - 1, True)
            for u in range(SLOTS):
                for g in range(STORES):
                    sp.wait_ge(group_stored[u][g], (PIECES // SLOTS) * DMA)

        @block.gpsimd
        def _(pool):
            nc.gpsimd.memset(zeros[:, :], 0.0).then_inc(cleared, 1)
            nc.gpsimd.memset(x_t[:, :, :, P:XT_ROW], 1.0).then_inc(cleared, 1)
            nc.gpsimd.memset(w_pair[:, :], 0.0).then_inc(cleared, 1)
            nc.gpsimd.memset(wt_pair[:, :], 0.0).then_inc(cleared, 1)
            nc.gpsimd.memset(score_w[:, :], 0.0).then_inc(cleared, 1)

        @block.tensor
        def _(pe):
            def open_or_close(sums, opens):
                return nc.tensor.matmul(sums, zeros[:, 0:P], zeros[:, 0:1].to_broadcast([P, sums.shape[-1]]),
                                        start=opens, stop=not opens, skip_group_check=True)

            def gram_tiles(h, first_tile):
                for u in range(IN_SLOTS):
                    at_least(pe, tile_turned, first_tile + u + 1)
                    for j in range(BLOCKS // 2):
                        two_blocks = x_t[:, u % XT_SLOTS, j, :]
                        last = nc.tensor.matmul(gram_ps[h], two_blocks[:, 0:P], two_blocks[:, 0:GW],
                                                start=False, stop=False, skip_group_check=True)
                    last.then_inc(tile_summed, 1)

            def image_gram(image):
                for h in range(2):
                    at_least(pe, gram_kept, image * 2 + h - 1)
                    open_or_close(gram_ps[h], True)
                    with pe.Fori(0, HALVES_ROUNDS[h]) as r:
                        gram_tiles(h, image * (ROUNDS * IN_SLOTS) + h * (HALVES_ROUNDS[0] * IN_SLOTS) + r * IN_SLOTS)
                    open_or_close(gram_ps[h], False).then_inc(gram_ended, 1)

            pe.wait_ge(cleared, 2)
            image_gram(0)
            with pe.Fori(1, B - 1) as image:
                image_gram(image)

            def add_parts(fours):
                pe.wait_ge(gram_kept, 2 * 4 * fours[-1] + 8)
                for q in fours:
                    for h in range(2):
                        last = nc.tensor.matmul(banks[:, 2 + q, 0:4 * G], same_channel,
                                                gram_kept_sb[:, 4 * q:4 * q + 4, h, :],
                                                start=(h == 0), stop=(h == 1))
                last.then_inc(pe_coef, 1)

            pe.wait_ge(masks_loaded, DMA)
            pe.wait_ge(weights_loaded, 6 * DMA)
            add_parts(range(B // 4 - 1))

            def sums_by_group(when, bank):
                first, end = PAIRS_OF[when]
                pe.wait_ge(dve_coef, dve_at["all_sum_sq_" + when])
                nc.tensor.matmul(banks[:, bank, 0:2 * (end - first)], same_group, sum_sq[:, :, first:end],
                                 start=True, stop=True).then_inc(pe_coef, 1)

            def through_conv(when, bank):
                first, end = PAIRS_OF[when]
                pe.wait_ge(dve_coef, dve_at["colsum_" + when])
                nc.tensor.matmul(banks[:, bank, 0:2 * (end - first)], wt_pair[:, :], conv_in[:, :, first:end],
                                 start=True, stop=True).then_inc(pe_coef, 1)

            def back_through_conv(when, bank):
                first, end = PAIRS_OF[when]
                pe.wait_ge(dve_coef, dve_at["cy_" + when])
                nc.tensor.matmul(banks[:, bank, 0:end - first], w_pair[:, :], cy[:, first:end],
                                 start=True, stop=True).then_inc(pe_coef, 1)

            def resident_scores(r, when):
                first, end = PAIRS_OF[when]
                for p in range(first, end):
                    for j in range(QUADS):
                        nc.tensor.matmul(resident_ps[r][j * QUAD:(j + 1) * QUAD, :],
                                         score_w[:, p * 2 * B:(p + 1) * 2 * B],
                                         piece_x[:, r, p, j * PART:(j + 1) * PART],
                                         start=False, stop=False, skip_group_check=True)
                if end == PAIRS and r % 2 == 1:
                    open_or_close(resident_banks[r // 2], False).then_inc(scores_summed, 2)

            last_image = B - 1
            rounds_done = 0
            for h in range(2):
                pe.wait_ge(gram_kept, last_image * 2 + h - 1)
                open_or_close(gram_ps[h], True)
                for _ in range(HALVES_ROUNDS[h]):
                    gram_tiles(h, (last_image * ROUNDS + rounds_done) * IN_SLOTS)
                    if rounds_done == 0:
                        sums_by_group("early", 2)
                    if rounds_done == 1:
                        through_conv("early", 3)
                    if rounds_done == 2:
                        back_through_conv("early", 4)
                    rounds_done += 1
                open_or_close(gram_ps[h], False).then_inc(gram_ended, 1)
            add_parts([B // 4 - 1])
            pe.wait_ge(dve_coef, dve_at["score_w_3_early"])
            for half in range(2):
                pe.wait_ge(resident_loaded[half], PAIRS * DMA)
            for sums in resident_banks:
                open_or_close(sums, True)
            resident_scores(0, "early")
            sums_by_group("late", 6)
            resident_scores(1, "early")
            through_conv("late", 7)
            back_through_conv("late", 6)
            resident_scores(2, "early")
            pe.wait_ge(dve_coef, dve_at["score_w_3_late"])
            for h in range(2):
                rows = slice(h * C, (h + 1) * C)
                for p in range(PAIRS):
                    last = nc.tensor.matmul(banks[rows, 4 + h, 2 * p:2 * p + 2], gram[rows, p, 0:C],
                                            sw[rows, :, p], start=True, stop=True)
            last.then_inc(pe_coef, 1)
            resident_scores(3, "early")
            pe.wait_ge(dve_coef, dve_at["part_forms_1"])
            nc.tensor.matmul(banks[:, 6, 0:6 * PAIRS], same_image, parts[:, :, :].rearrange("q t p -> q (t p)"),
                             start=True, stop=True).then_inc(pe_coef, 1)
            resident_scores(0, "late")
            resident_scores(1, "late")
            pe.wait_ge(dve_coef, dve_at["norm2"])
            for h in range(2):
                last = nc.tensor.matmul(banks[:, 7, 4 * PAIRS * h:4 * PAIRS * (h + 1)], row_of_image[h],
                                        to_rows[:, :, :, :].rearrange("q a t p -> q (a t p)"), start=True, stop=True)
            last.then_inc(pe_coef, 1)
            resident_scores(2, "late")
            resident_scores(3, "late")
            pe.wait_ge(dve_coef, dve_at["all_rows"])
            for a in range(2):
                last = nc.tensor.matmul(banks[:, 4, a:a + 1], all_rows[:, a, :, :].rearrange("q j r -> q (j r)"),
                                        first_row, start=True, stop=True)
            last.then_inc(pe_coef, 1)
            pe.wait_ge(resident_squared, SLOTS)
            nc.tensor.matmul(banks[:, 0, 0:SLOTS], same_score, resident_norm[:, :],
                             start=True, stop=True).then_inc(pe_coef, 1)

            def conv(i, u, p):
                n = u * PAIRS + p
                for k in range(HALVES):
                    at_least(pe, y_ready, i * (SLOTS * PAIRS * HALVES) + (n - 1) * HALVES + k + 1)
                    nc.tensor.matmul(y_ps[k], conv_w[:, p, :], x_of(i, u, p)[:, k * BANK:(k + 1) * BANK],
                                     start=True, stop=True).then_inc(conv_done, 1)

            def sum_scores(i, u, pairs):
                if pairs[0] == 0:
                    at_least(pe, piece_loaded[u % SLOTS], i * (STORES * DMA) + STORES * DMA * (u // SLOTS))
                    at_least(pe, rows_ready, i * SLOTS + u)
                for p in pairs:
                    for j in range(QUADS):
                        last = nc.tensor.matmul(scores_ps[j * QUAD:(j + 1) * QUAD, :],
                                                score_w[:, p * 2 * B:(p + 1) * 2 * B],
                                                x_of(i, u, p)[:, j * PART:(j + 1) * PART],
                                                start=(p == 0), stop=(p == PAIRS - 1))
                if pairs[-1] == PAIRS - 1:
                    last.then_inc(scores_summed, 1)

            def pieces(i, last_pieces):
                for u in range(SLOTS):
                    for p in range(PAIRS):
                        n = u * PAIRS + p
                        if not (isinstance(i, int) and i == 0 and n < EARLY_Y):
                            conv(i, u, p)
                        if p == 0:
                            at_least(pe, gate_ready, i * SLOTS + u + 1)
                        at_least(pe, gated, i * (SLOTS * PAIRS) + n - 1)
                        for j in range(QUADS):
                            last = nc.tensor.matmul(gate_ps[n % 2][:, j * PART:(j + 1) * PART], select[:, j, p, :],
                                                    gate_rows[:, u % 2, :], start=True, stop=True)
                        last.then_inc(gate_spread, 1)
                        resident = isinstance(i, int) and i == 0 and u + 1 < SLOTS
                        if p in SCORES_AFTER and not (last_pieces and u == SLOTS - 1) and not resident:
                            sum_scores(i, u + 1, SCORES_AFTER[p])

            pe.wait_ge(act_coef, act_at["conv_w_late"])
            for p in range(EARLY_Y):
                conv(0, 0, p)
            pe.wait_ge(select_loaded, DMA)
            pieces(0, False)
            pieces(1, False)
            with pe.Fori(2, PIECES // SLOTS - 1) as i:
                pieces(i, False)
            pieces(PIECES // SLOTS - 1, True)

        @block.scalar
        def _(act):
            def keep_gram(image):
                for h in range(2):
                    act.wait_ge(gram_ended, image * 2 + h + 1)
                    kept = gram_kept_sb[:, bass.ds(image, 1), h, :].rearrange("q b g -> q (b g)")
                    nc.scalar.copy(kept[0:C, 0:C], gram_ps[h][0:C, 0:C])
                    nc.scalar.copy(kept[0:C, C:G], gram_ps[h][0:C, 2 * C:GW])
                    nc.scalar.copy(kept[C:P, :], gram_ps[h][C:P, C:GW]).then_inc(gram_kept, 1)

            def sum_resident(pair):
                for h in range(2):
                    act.wait_ge(resident_loaded[h], pair * DMA + DMA)
                for r in range(SLOTS):
                    for k, func in enumerate((ACT.Copy, ACT.Square)):
                        at_least(act, resident_summed, pair * (2 * SLOTS) + 2 * r + k)
                        nc.scalar.activation(
                            unused_ps, piece_x[:, r, bass.ds(pair, 1), :].rearrange("q p n -> q (p n)"), func,
                            accum_out=resident_stats[:, k, bass.ds(pair, 1), r]).then_inc(resident_summed, 1)

            keep_gram(0)
            sum_resident(0)
            keep_gram(1)
            with act.Fori(1, PAIRS - 1) as pair:
                keep_gram(pair * 2)
                sum_resident(pair)
                keep_gram(pair * 2 + 1)

            def conv_weights(when):
                first, end = PAIRS_OF[when]
                act.wait_ge(dve_coef, dve_at["var_eps_" + when])
                nc.scalar.activation(std[:, first:end], var[:, first:end], ACT.Sqrt).then_inc(act_coef, 1)
                act.wait_ge(dve_coef, dve_at["rstd_" + when])
                act.wait_ge(weights_loaded, 6 * DMA)
                for p in range(first, end):
                    last = nc.scalar.activation(conv_w[:, p, :], wt_pair[:, :], ACT.Copy, scale=rstd[:, p:p + 1])
                last.then_inc(act_coef, 1)

            keep_gram(B - 2)
            conv_weights("early")
            sum_resident(PAIRS - 1)
            keep_gram(B - 1)
            conv_weights("late")
            for r in range(SLOTS):
                act.wait_ge(scores_summed, r + 1)
                nc.scalar.copy(resident_rows[:, r, :], resident_ps[r]).then_inc(resident_out, 1)
                act.wait_ge(resident_out, r + 1)
                at_least(act, resident_squared, r)
                nc.scalar.activation(unused_rows_ps, resident_rows[:, r, :], ACT.Square,
                                     accum_out=resident_norm[:, r:r + 1]).then_inc(resident_squared, 1)
            act.wait_ge(dve_coef, dve_at["row_held"])
            nc.scalar.activation(row_norm[:, :], row_norm2[:, :], ACT.Sqrt).then_inc(act_coef, 1)

            def score_rows_out(n):
                if isinstance(n, int) and n < SLOTS:
                    scores_from = resident_rows[:, n, :]
                else:
                    act.wait_ge(scores_summed, n + 1)
                    scores_from = scores_ps
                at_least(act, scores_turned, n)
                nc.scalar.activation(score_rows[:, :], scores_from, ACT.Identity, bias=row_b[:, 0:1],
                                     scale=row_inv[:, 0:1]).then_inc(rows_ready, 1)

            def exponentials(n):
                at_least(act, scores_ready, n + 1)
                nc.scalar.activation(e_sb[:, :, :], diff_sb[:, :, :], ACT.Exp).then_inc(exp_ready, 1)

            def gate_out(n):
                at_least(act, soft, n * 4 + 4)
                nc.scalar.activation(tanh_sb[:, :, :], g_sb[:, :, :], ACT.Tanh, scale=0.5).then_inc(tanh_ready, 1)
                at_least(act, tanh_ready, n + 1)
                nc.scalar.activation(gate_parts[:, :, 0:B], tanh_sb[:, :, :], ACT.Copy, bias=ATT_SCALE / 2,
                                     scale=ATT_SCALE / 2).then_inc(high_ready, 1)

            def y_out(i, n, p, k):
                at_least(act, conv_done, i * (SLOTS * PAIRS * HALVES) + n * HALVES + k + 1)
                nc.scalar.activation(y_sb[:, n % Y_SLOTS, k * BANK:(k + 1) * BANK], y_ps[k], ACT.Identity,
                                     bias=conv_b[:, p:p + 1], scale=1.0).then_inc(y_ready, 1)

            def pieces(i, last_pieces):
                for u in range(SLOTS):
                    following = i * SLOTS + u + 1
                    more = not (last_pieces and u == SLOTS - 1)
                    for p in range(PAIRS):
                        n = u * PAIRS + p
                        if not (isinstance(i, int) and i == 0 and n < EARLY_Y):
                            at_least(act, added, i * (SLOTS * PAIRS) + n + 1 - Y_SLOTS)
                            for k in range(HALVES):
                                y_out(i, n, p, k)
                        if more and p == ROWS_AFTER:
                            score_rows_out(following)
                        if more and p == EXP_AFTER:
                            exponentials(following)
                        if more and p == TANH_AFTER:
                            gate_out(following)

            nc.scalar.activation(unused_col[:, :], conv_b[:, 0:1], ACT.Tanh)
            act.wait_ge(tile_summed, B * ROUNDS * IN_SLOTS)
            y_out(0, 0, 0, 0)
            y_out(0, 0, 0, 1)
            act.wait_ge(dve_coef, dve_at["row_b"])
            score_rows_out(0)
            y_out(0, 1, 1, 0)
            exponentials(0)
            y_out(0, 1, 1, 1)
            gate_out(0)
            pieces(0, False)
            with act.Fori(1, PIECES // SLOTS - 1) as i:
                pieces(i, False)
            pieces(PIECES // SLOTS - 1, True)

        @block.vector
        def _(dve):
            def turn_round(rnd):
                for u in range(IN_SLOTS):
                    at_least(dve, tile_loaded[u], rnd * (QUADS * DMA) + QUADS * DMA)
                    at_least(dve, tile_summed, rnd * IN_SLOTS + u + 1 - XT_SLOTS)
                    nc.vector.transpose(
                        x_t[:, u % XT_SLOTS, :, 0:P].rearrange("q j (d e c) -> q j d e c", d=2, e=CH),
                        tiles_in[:, u, :, :].rearrange("q e (j d n) -> q j d e n", d=2, n=QUAD)).then_inc(tile_turned, 1)

            done = []

            def step(name, instruction):
                done.append(name)
                assert DVE_STEPS[len(done) - 1] == name
                instruction.then_inc(dve_coef, 1)
                dve.wait_ge(dve_coef, len(done))

            tt, ts, stt = nc.vector.tensor_tensor, nc.vector.tensor_scalar, nc.vector.scalar_tensor_tensor

            def take_grams(when):
                first, end = PAIRS_OF[when]
                dve.wait_ge(pe_coef, pe_at["gram_" + when])
                pairs = slice(first, end)
                for h in range(2):
                    rows = slice(h * C, (h + 1) * C)
                    src = banks[rows, 2 + first // 2:2 + end // 2, 0:4 * G].rearrange(
                        "q a (e h g) -> q a e h g", h=2, g=G)
                    step(f"gram_{h}_{when}", nc.vector.tensor_copy(
                        gram[rows, pairs, :].rearrange("q (a e) g -> q a e g", e=2), src[:, :, :, h, :]))
                step("diag_" + when, tt(gram_diag[:, pairs, :], gram[:, pairs, 0:C],
                                        eye.unsqueeze(1).to_broadcast([P, end - first, C]), ALU.mult))
                step("sums_" + when, nc.vector.tensor_copy(sum_sq[:, 0, pairs], gram[:, pairs, C]))
                step("squares_" + when, nc.vector.tensor_reduce(sum_sq[:, 1, pairs], gram_diag[:, pairs, :],
                                                                AX_X, ALU.add))
                dve.wait_ge(resident_summed, end * 2 * SLOTS)
                step("resident_sum_sq_" + when, nc.vector.tensor_reduce(
                    resident_sum_sq[:, :, pairs], resident_stats[:, :, pairs, :], AX_X, ALU.add))
                step("all_sum_sq_" + when, tt(sum_sq[:, :, pairs], sum_sq[:, :, pairs], resident_sum_sq[:, :, pairs],
                                              ALU.add))

            def inverse_root(first, names, root, value, scratch, result):
                step(names[0], nc.vector.reciprocal(first, root))
                step(names[1], tt(scratch, first, first, ALU.mult))
                step(names[2], tt(scratch, scratch, value, ALU.mult))
                step(names[3], ts(scratch, scratch, -0.5, 1.5, ALU.mult, ALU.add))
                step(names[4], tt(result, first, scratch, ALU.mult))

            def normed(when, bank):
                first, end = PAIRS_OF[when]
                pairs = slice(first, end)
                dve.wait_ge(pe_coef, pe_at["groups_" + when])
                step("mean_sq_" + when, ts(mean_sq[:, :, pairs],
                                           banks[:, bank, 0:2 * (end - first)].rearrange("q (t p) -> q t p", t=2),
                                           1.0 / (2 * N), None, ALU.mult))
                step("mean2_" + when, tt(newton[:, 0, pairs], mean[:, pairs], mean[:, pairs], ALU.mult))
                step("var_" + when, tt(var[:, pairs], mean_sq[:, 1, pairs], newton[:, 0, pairs], ALU.subtract))
                step("var_eps_" + when, ts(var[:, pairs], var[:, pairs], 0.0, GN_EPS, ALU.max, ALU.add))
                dve.wait_ge(act_coef, act_at["std_" + when])
                inverse_root(rstd0[:, pairs], [name + "_" + when for name in ("rstd0", "r_sq", "r_sq_v", "r_fix", "rstd")],
                             std[:, pairs], var[:, pairs], newton[:, 0, pairs], rstd[:, pairs])
                step("rm_" + when, tt(conv_in[:, 1, pairs], rstd[:, pairs], mean[:, pairs], ALU.mult))
                step("centred_" + when, stt(out=newton[:, 1, pairs], in0=mean[:, pairs], scalar=-float(N),
                                            in1=sum_sq[:, 0, pairs], op0=ALU.mult, op1=ALU.add))
                step("colsum_" + when, tt(conv_in[:, 0, pairs], newton[:, 1, pairs], rstd[:, pairs], ALU.mult))

            def convolved(when, bank):
                first, end = PAIRS_OF[when]
                pairs = slice(first, end)
                dve.wait_ge(pe_coef, pe_at["conv_" + when])
                step("cy_" + when, ts(cy[:, pairs], banks[:, bank, 0:end - first], b_times_n[:, 0:1], None, ALU.add))
                step("conv_b_" + when, ts(conv_b[:, pairs], banks[:, bank, end - first:2 * (end - first)], -1.0,
                                          b_col[:, 0:1], ALU.mult, ALU.add))
                step("sw_x_" + when, tt(sw[:, 0, pairs], conv_in[:, 0, pairs], rstd[:, pairs], ALU.mult))

            def score_weights(when, bank):
                first, end = PAIRS_OF[when]
                pairs = slice(first, end)
                dve.wait_ge(pe_coef, pe_at["back_" + when])
                step("sw_y_" + when, tt(sw[:, 1, pairs], banks[:, bank, 0:end - first], rstd[:, pairs], ALU.mult))
                dve.wait_ge(cleared, 5)
                stride = 2 * B + 2
                for t in range(2):
                    for h in range(2):
                        rows, at = slice(h * C, (h + 1) * C), t * B + h
                        step(f"score_w_{2 * t + h}_{when}", nc.vector.tensor_copy(
                            score_w[rows, first * stride + at:min(end * stride + at, PAIRS * 2 * B):stride],
                            sw[rows, t, pairs]))

            turn_round(0)
            with dve.Fori(1, (B - 1) * ROUNDS) as rnd:
                turn_round(rnd)
            turn_round((B - 1) * ROUNDS)
            dve.wait_ge(weights_loaded, 6 * DMA)
            dve.wait_ge(masks_loaded, DMA)
            step("b_times_n", ts(b_times_n[:, :], b_col[:, :], float(N), None, ALU.mult))
            take_grams("early")
            turn_round((B - 1) * ROUNDS + 1)
            normed("early", 2)
            turn_round((B - 1) * ROUNDS + 2)
            convolved("early", 3)
            turn_round((B - 1) * ROUNDS + 3)
            score_weights("early", 4)
            with dve.Fori((B - 1) * ROUNDS + 4, B * ROUNDS) as rnd:
                turn_round(rnd)
            take_grams("late")
            normed("late", 6)
            convolved("late", 7)
            score_weights("late", 6)
            step("part_0", tt(parts[:, 0, :], sw[:, 0, :], mean, ALU.mult))
            step("part_1", tt(parts[:, 1, :], cy[:, :], conv_b[:, :], ALU.mult))
            step("part_sums", tt(parts[:, 2:4, :], sw[:, :, :],
                                 sum_sq[:, 0, :].unsqueeze(1).to_broadcast([P, 2, PAIRS]), ALU.mult))
            dve.wait_ge(pe_coef, pe_at["forms"])
            for h in range(2):
                rows = slice(h * C, (h + 1) * C)
                step(f"part_forms_{h}", tt(parts[rows, 4:6, :], sw[rows, :, :],
                                           banks[rows, 4 + h, 0:2 * PAIRS].rearrange("q (p t) -> q t p", t=2),
                                           ALU.mult))
            dve.wait_ge(pe_coef, pe_at["totals"])
            step("totals", nc.vector.tensor_copy(totals[:, :, :].rearrange("q t p -> q (t p)"),
                                                 banks[:, 6, 0:6 * PAIRS]))
            step("sk_x", ts(sk[:, 0, :], totals[:, 0, :], -1.0, None, ALU.mult))
            step("sk_y", nc.vector.tensor_copy(sk[:, 1, :], totals[:, 1, :]))
            step("sk_sq", tt(sk_sq[:, :, :], sk, sk, ALU.mult))
            step("cross", tt(cross[:, :, :], sk, totals[:, 2:4, :], ALU.mult))
            step("cross2", stt(out=cross[:, :, :], in0=cross[:, :, :], scalar=2.0, in1=totals[:, 4:6, :],
                               op0=ALU.mult, op1=ALU.add))
            step("norm2", stt(out=norm2, in0=sk_sq[:, :, :], scalar=float(N), in1=cross[:, :, :],
                              op0=ALU.mult, op1=ALU.add))
            dve.wait_ge(pe_coef, pe_at["one_row"])
            for a in range(2):
                src = banks[:, 7, 0:4 * B].rearrange("q (h a t p) -> q a t p h", h=2, a=2, t=2)
                step(f"one_row_{a}", nc.vector.tensor_copy(
                    one_row[:, a, :].rearrange("q (t p h) -> q t p h", t=2, h=2), src[:, a, :, :, :]))
            step("all_rows", nc.vector.tensor_copy(all_rows[:, :, :, :],
                                                   one_row[:, :, :].unsqueeze(2).to_broadcast([P, 2, QUADS, 2 * B])))
            dve.wait_ge(pe_coef, pe_at["rows"])
            step("row_k", nc.vector.tensor_copy(row_k[:, :], banks[:, 4, 1:2]))
            dve.wait_ge(pe_coef, pe_at["resident"])
            step("row_resident", nc.vector.tensor_reduce(row_resident[:, :], banks[:, 0, 0:SLOTS], AX_X, ALU.add))
            step("row_norm2", tt(row_norm2[:, :], row_resident[:, :], banks[:, 4, 0:1], ALU.add))
            step("row_held", ts(row_norm2[:, :], row_norm2[:, :], NORM_EPS ** 2, None, ALU.max))
            dve.wait_ge(act_coef, act_at["row_norm"])
            inverse_root(row_inv0[:, :], ["inv0", "i_sq", "i_sq_n", "i_fix", "row_inv"], row_norm[:, :],
                         row_norm2[:, :], row_fix[:, :], row_inv[:, :])
            step("row_b", tt(row_b[:, :], row_k[:, :], row_inv[:, :], ALU.mult))

            def scores_by_pixel(n):
                at_least(dve, rows_ready, n + 1)
                nc.vector.transpose(scores[:, :, :].rearrange("q i r -> q (i r)"),
                                    score_rows[:, :]).then_inc(scores_turned, 1)
                dve.wait_ge(scores_turned, n + 1)
                tt(diff_sb[:, :, :], scores[:, :, B:2 * B], scores[:, :, 0:B], ALU.subtract).then_inc(scores_ready, 1)

            def softmax(n):
                at_least(dve, exp_ready, n + 1)
                nc.vector.tensor_reduce(z_sb[:, :], e_sb[:, :, :], AX_X, ALU.add).then_inc(soft, 1)
                at_least(dve, soft, n * 4 + 1)
                nc.vector.reciprocal(rz_sb[:, :], z_sb[:, :]).then_inc(soft, 1)
                at_least(dve, soft, n * 4 + 2)
                tt(p_sb[:, :, :], e_sb[:, :, :], rz_sb[:, :].unsqueeze(2).to_broadcast([P, PB, B]),
                   ALU.mult).then_inc(soft, 1)
                at_least(dve, soft, n * 4 + 3)
                stt(out=g_sb[:, :, :], in0=p_sb[:, :, :], scalar=1.0, in1=scores[:, :, B:2 * B],
                    op0=ALU.add, op1=ALU.mult).then_inc(soft, 1)

            def whole_gate(n):
                at_least(dve, tanh_ready, n + 1)
                ts(gate4k[:, :, :], tanh_sb[:, :, :], ATT_SCALE / 2, ATT_SCALE / 2,
                   ALU.mult, ALU.add).then_inc(split, 1)

            def gate_by_row(n, parity):
                at_least(dve, split, n * 2 + 1)
                at_least(dve, high_ready, n + 1)
                tt(gate_parts[:, :, B:2 * B], gate4k[:, :, :], gate_parts[:, :, 0:B],
                   ALU.subtract).then_inc(split, 1)
                at_least(dve, split, n * 2 + 2)
                nc.vector.transpose(gate_rows[:, parity, :],
                                    gate_parts[:, :, :].rearrange("q i r -> q (i r)")).then_inc(gate_ready, 1)

            def pieces(i, last_pieces):
                for u in range(SLOTS):
                    following = i * SLOTS + u + 1
                    more = not (last_pieces and u == SLOTS - 1)

                    def gate(p):
                        n = u * PAIRS + p
                        at_least(dve, y_ready, i * (SLOTS * PAIRS * HALVES) + (n + 1) * HALVES)
                        at_least(dve, gate_spread, i * (SLOTS * PAIRS) + n + 1)
                        tt(y_sb[:, n % Y_SLOTS, :], y_sb[:, n % Y_SLOTS, :], gate_ps[n % 2], ALU.mult).then_inc(gated, 1)

                    def add(p):
                        n = u * PAIRS + p
                        at_least(dve, gated, i * (SLOTS * PAIRS) + n + 1)
                        tt(x_of(i, u, p), y_sb[:, n % Y_SLOTS, :], x_of(i, u, p), ALU.add).then_inc(added, 1)

                    for p in range(PAIRS):
                        gate(p)
                        if p > 0:
                            add(p - 1)
                        if more and p == TURN_AFTER:
                            scores_by_pixel(following)
                        if more and p == SOFTMAX_AFTER:
                            softmax(following)
                        if more and p == GATE_AFTER:
                            whole_gate(following)
                            gate_by_row(following, (u + 1) % 2)
                    add(PAIRS - 1)

            scores_by_pixel(0)
            softmax(0)
            whole_gate(0)
            gate_by_row(0, 0)
            pieces(0, False)
            pieces(1, False)
            with dve.Fori(2, PIECES // SLOTS - 1) as i:
                pieces(i, False)
            pieces(PIECES // SLOTS - 1, True)


def masks_of_shape(np, B, C):
    P, QUAD = 128, 32
    row, col = np.arange(P)[:, None], np.arange(P)[None, :]
    eye = (row % C == np.arange(C)[None, :])
    same_channel = row % C == col % C
    same_group = row // 2 == col // 2
    same_image = row // C == col // C
    rows = [np.broadcast_to(row == h * C, (P, P)) for h in range(2)]
    same_score = row % QUAD == col % QUAD
    masks = np.concatenate([eye, same_channel, same_group, same_image, *rows, same_score, row == 0], axis=1)
    select = np.zeros((P, P // QUAD, B // 2, P), np.float16)
    for j in range(P // QUAD):
        for p in range(B // 2):
            for h in range(2):
                for part in range(2):
                    select[j * QUAD + part * B + 2 * p + h, j, p, h * C:(h + 1) * C] = 1.0 / 4096.0
    return masks.astype(np.float32), select.reshape(P, -1)


def kernel(**inputs):
    import numpy as _np
    import concourse.bacc as _bacc
    from concourse import mybir as _mybir
    from concourse.bass_utils import run_bass_kernel_spmd as _run

    nc = _bacc.Bacc("TRN2", target_bir_lowering=False, num_devices=1)
    x = _np.ascontiguousarray(inputs["x"])
    w = _np.ascontiguousarray(inputs["L0_conv_pw_w"])
    masks, select = masks_of_shape(_np, x.shape[0], x.shape[1])
    arrays = {
        "in_x": x,
        "in_w": w,
        "in_w_t": _np.ascontiguousarray(w.T),
        "in_b": _np.ascontiguousarray(inputs["L0_conv_pw_b"]).reshape(-1, 1),
        "in_masks": masks,
        "in_select": select,
    }
    args = [nc.dram_tensor(n, a.shape, _mybir.dt.from_np(a.dtype), kind="ExternalInput").ap()
            for n, a in arrays.items()]
    out = nc.dram_tensor("out_0", x.shape, _mybir.dt.from_np(x.dtype), kind="ExternalOutput").ap()
    build_kernel(nc, *args, out)
    r = _run(nc, [arrays], core_ids=[0])
    return r.results[0]["out_0"]
```
